# Optimizing a Trainium2 kernel written in Bass

```python
import numpy as np
import jax
import jax.numpy as jnp

def _softmax(x, axis=-1):
    return jax.nn.softmax(x, axis=axis)

def _gelu(x):
    return jax.nn.gelu(x, approximate=True)

def _silu(x):
    return jax.nn.silu(x)

def _sigmoid(x):
    return jax.nn.sigmoid(x)

def _layernorm(x, axis=-1, eps=1e-05):
    m = jnp.mean(x, axis=axis, keepdims=True)
    v = jnp.var(x, axis=axis, keepdims=True)
    return (x - m) / jnp.sqrt(v + eps)

def _scatter_add(tgt, idx, src, axis=0):
    return tgt.at[idx].add(src)

def _segment_sum(src, seg, n):
    return jax.ops.segment_sum(src, seg, n)
kernel_name = 'mk_adj_resnorm_d2_adj_r2_c38565'

def setup_inputs(seed: int=0):
    np.random.seed(seed)
    _w = jnp.asarray

    def _rec_inputs():
        import jax
        import jax.numpy as jnp
        _gk = jax.random.key(seed)
        x = -0.0001538 + 1 * jax.random.normal(jax.random.fold_in(_gk, 1), (64, 128, 384), jnp.float32)
        _a = jax.random.bernoulli(jax.random.fold_in(_gk, 2), 0.03125, (64, 128, 128))
        _a = jnp.logical_or(_a, jnp.swapaxes(_a, -1, -2))
        _a = jnp.logical_or(_a, jnp.eye(128, dtype=bool))
        adj = _a
        return (x, adj)
    x, adj = _rec_inputs()

    def _L0_gnn_setup():
        import jax, jax.numpy as jnp
        import numpy as np
        B, S, H = (4, 1024, 384)
        NUM_HEADS = 6
        HEAD_SIZE = H // NUM_HEADS
        NEG = -9000000000000000.0

        def _heads(x):
            b, s, _ = x.shape
            return x.reshape(b, s, NUM_HEADS, HEAD_SIZE).transpose(0, 2, 1, 3)
        key = jax.random.key(seed)
        ks = jax.random.split(key, 10)
        seq_inputs = jax.random.normal(ks[0], (B, S, H), dtype=jnp.float32)
        gm = jax.random.randint(ks[1], (B, S, S), 0, 2) > 0
        graph_mask = gm | jnp.eye(S, dtype=bool)[None]
        sc = 1.0 / np.sqrt(H)
        Wq = jax.random.normal(ks[2], (H, H), dtype=jnp.float32) * sc
        bq = jnp.zeros((H,), dtype=jnp.float32)
        Wk = jax.random.normal(ks[3], (H, H), dtype=jnp.float32) * sc
        bk = jnp.zeros((H,), dtype=jnp.float32)
        Wv = jax.random.normal(ks[4], (H, H), dtype=jnp.float32) * sc
        bv = jnp.zeros((H,), dtype=jnp.float32)
        Wf = jax.random.normal(ks[5], (H, H), dtype=jnp.float32) * sc
        bf = jnp.zeros((H,), dtype=jnp.float32)
        return {'seq_inputs': seq_inputs, 'Wq': Wq, 'bq': bq, 'Wk': Wk, 'bk': bk, 'Wv': Wv, 'bv': bv, 'Wf': Wf, 'bf': bf, 'graph_mask': graph_mask}
    _L0_gnn_all = _L0_gnn_setup()
    _L0_gnn_in = {k: v for k, v in _L0_gnn_all.items() if k in ('Wq', 'bq', 'Wk', 'bk', 'Wv', 'bv', 'Wf', 'bf')}
    del _L0_gnn_all

    def _L1_gnn_setup():
        import jax, jax.numpy as jnp
        import numpy as np
        ATT_HEAD = 12
        IN_DIM = 384
        OUT_DIM = IN_DIM // ATT_HEAD
        LEAKY_ALPHA = 0.2
        B, N = (8, 256)
        key = jax.random.key(seed)
        ks = jax.random.split(key, 8)
        feat_in = jax.random.normal(ks[0], (B, N, IN_DIM), dtype=jnp.float32)
        adj = jax.random.randint(ks[1], (B, N, N), 0, 2) > 0
        lim_W = float(np.sqrt(6.0 / (IN_DIM + OUT_DIM)))
        W = jax.random.uniform(ks[2], (ATT_HEAD, IN_DIM, OUT_DIM), minval=-lim_W, maxval=lim_W, dtype=jnp.float32)
        b = jnp.zeros((OUT_DIM,), dtype=jnp.float32)
        lim_w = float(np.sqrt(6.0 / (OUT_DIM + 1)))
        w_src = jax.random.uniform(ks[3], (ATT_HEAD, OUT_DIM, 1), minval=-lim_w, maxval=lim_w, dtype=jnp.float32)
        w_dst = jax.random.uniform(ks[4], (ATT_HEAD, OUT_DIM, 1), minval=-lim_w, maxval=lim_w, dtype=jnp.float32)
        std_H = float(np.sqrt(2.0 / (IN_DIM + IN_DIM)))
        H_w = jax.random.normal(ks[5], (IN_DIM, IN_DIM), dtype=jnp.float32) * std_H
        H_b = jax.random.normal(ks[6], (IN_DIM,), dtype=jnp.float32) * 0.01
        return {'feat_in': feat_in, 'adj': adj, 'W': W, 'b': b, 'w_src': w_src, 'w_dst': w_dst, 'H_w': H_w, 'H_b': H_b}
    _L1_gnn_all = _L1_gnn_setup()
    _L1_gnn_in = {k: v for k, v in _L1_gnn_all.items() if k in ('W', 'b', 'w_src', 'w_dst', 'H_w', 'H_b')}
    del _L1_gnn_all
    return {'x': x, 'adj': adj, 'L0_gnn_Wq': _L0_gnn_in['Wq'], 'L0_gnn_bq': _L0_gnn_in['bq'], 'L0_gnn_Wk': _L0_gnn_in['Wk'], 'L0_gnn_bk': _L0_gnn_in['bk'], 'L0_gnn_Wv': _L0_gnn_in['Wv'], 'L0_gnn_bv': _L0_gnn_in['bv'], 'L0_gnn_Wf': _L0_gnn_in['Wf'], 'L0_gnn_bf': _L0_gnn_in['bf'], 'L1_gnn_W': _L1_gnn_in['W'], 'L1_gnn_b': _L1_gnn_in['b'], 'L1_gnn_w_src': _L1_gnn_in['w_src'], 'L1_gnn_w_dst': _L1_gnn_in['w_dst'], 'L1_gnn_H_w': _L1_gnn_in['H_w'], 'L1_gnn_H_b': _L1_gnn_in['H_b']}

def reference(x, adj, L0_gnn_Wq, L0_gnn_bq, L0_gnn_Wk, L0_gnn_bk, L0_gnn_Wv, L0_gnn_bv, L0_gnn_Wf, L0_gnn_bf, L1_gnn_W, L1_gnn_b, L1_gnn_w_src, L1_gnn_w_dst, L1_gnn_H_w, L1_gnn_H_b):
    import jax
    import jax.numpy as jnp

    def _L0_gnn_ref(seq_inputs, Wq, bq, Wk, bk, Wv, bv, Wf, bf, graph_mask):
        import jax, jax.numpy as jnp
        import numpy as np
        B, S, H = (4, 1024, 384)
        NUM_HEADS = 6
        HEAD_SIZE = H // NUM_HEADS
        NEG = -9000000000000000.0

        def _heads(x):
            b, s, _ = x.shape
            return x.reshape(b, s, NUM_HEADS, HEAD_SIZE).transpose(0, 2, 1, 3)
        q = _heads(seq_inputs @ Wq + bq)
        k = _heads(seq_inputs @ Wk + bk)
        v = _heads(seq_inputs @ Wv + bv)
        scores = jnp.einsum('bhqd,bhkd->bhqk', q, k) / np.sqrt(HEAD_SIZE)
        bias = jnp.where(graph_mask, 0.0, NEG)[:, None]
        probs = jax.nn.softmax(scores + bias, axis=-1)
        ctx = jnp.einsum('bhqk,bhkd->bhqd', probs, v)
        ctx = ctx.transpose(0, 2, 1, 3).reshape(seq_inputs.shape[0], seq_inputs.shape[1], H)
        return ctx @ Wf + bf

    def _L1_gnn_ref(feat_in, adj, W, b, w_src, w_dst, H_w, H_b):
        import jax, jax.numpy as jnp
        import numpy as np
        ATT_HEAD = 12
        IN_DIM = 384
        OUT_DIM = IN_DIM // ATT_HEAD
        LEAKY_ALPHA = 0.2
        B, N = (8, 256)
        h = jnp.einsum('bnd,ade->bane', feat_in, W)
        th = jnp.tanh(h)
        attn_src = jnp.einsum('bane,aeo->bano', th, w_src)
        attn_dst = jnp.einsum('bane,aeo->bano', th, w_dst)
        attn = attn_src + jnp.swapaxes(attn_dst, 2, 3)
        attn = jnp.where(attn >= 0, attn, LEAKY_ALPHA * attn)
        mask = ~adj[:, None, :, :]
        attn = jnp.where(mask, jnp.float32(-999.0), attn)
        attn = jax.nn.softmax(attn, axis=-1)
        feat_out = jnp.einsum('banm,bame->bane', attn, h) + b
        feat_out = jnp.swapaxes(feat_out, 1, 2).reshape(feat_in.shape[0], feat_in.shape[1], -1)
        feat_out = jax.nn.elu(feat_out)
        gate = jax.nn.sigmoid(feat_in @ H_w.T + H_b)
        return gate * feat_out + (1.0 - gate) * feat_in
    x = _layernorm(x + _L0_gnn_ref(x, L0_gnn_Wq, L0_gnn_bq, L0_gnn_Wk, L0_gnn_bk, L0_gnn_Wv, L0_gnn_bv, L0_gnn_Wf, L0_gnn_bf, adj), axis=-1)
    x = _layernorm(x + _L1_gnn_ref(x, adj, L1_gnn_W, L1_gnn_b, L1_gnn_w_src, L1_gnn_w_dst, L1_gnn_H_w, L1_gnn_H_b), axis=-1)
    return x

_drawn_inputs = setup_inputs


def setup_inputs(seed=0):
    import zlib

    import numpy as np

    out = dict(_drawn_inputs(seed))
    spreads = {'L0_gnn_bq': (0.0, 0.1),
     'L0_gnn_bk': (0.0, 2.0),
     'L0_gnn_bv': (0.0, 0.1),
     'L0_gnn_bf': (0.0, 0.1),
     'L1_gnn_b': (0.0, 0.1)}
    factors = {'L1_gnn_H_b': 34.214}
    for name, (base, spread) in spreads.items():
        noise = np.random.default_rng([zlib.crc32(name.encode()), seed]).standard_normal(out[name].shape)
        drawn = base * np.exp(spread * noise) if base else spread * noise
        out[name] = jnp.asarray(drawn.astype(out[name].dtype))
    for name, factor in factors.items():
        out[name] = (out[name] * factor).astype(out[name].dtype)
    return out
```

```python
from contextlib import ExitStack

import concourse.bass as bass
from concourse import mybir

F32 = mybir.dt.float32
F32R = mybir.dt.float32r
BF16 = mybir.dt.bfloat16
U8 = mybir.dt.uint8
ALU = mybir.AluOpType
ACT = mybir.ActivationFunctionType
AX_X = mybir.AxisListType.X

P = 128
GROUP = 4
MASKED = -(2.0 ** 56)
LN_EPS = 1e-5
LEAKY = 0.2
EXP_ROOM = 80.0
KEEP, FLOOR = 1e37, 1e-30

PE_ORDER = [
    ("xT", 0), ("xT", 1), ("x1T", 0), ("xT", 2), ("xT", 3),
    ("h", 0), ("qk", 0), ("gate", 0), ("qk", 1), ("x1T", 1), ("wb", 0), ("h", 1), ("qk", 2), ("qk", 3),
    ("gate", 1), ("pv1", 0), ("x1T", 2), ("h", 2), ("wb", 1), ("qk", 4), ("qk", 5),
    ("s", 0), ("v", 0), ("x1T", 3), ("v", 1), ("st", 0), ("gate", 2), ("s", 1), ("pv1", 1), ("pv0", 0), ("wb", 2),
    ("h", 3), ("st", 1), ("cT", 0), ("v", 2), ("s", 2), ("pv0", 1), ("f", 0), ("wb", 3), ("st", 2), ("cT", 1),
    ("pv1", 2), ("s", 3), ("pv0", 2), ("f", 1), ("v", 3), ("st", 3), ("cT", 2), ("gate", 3), ("pv0", 3), ("f", 2),
    ("pv1", 3), ("maskT", 0), ("maskT", 1), ("cT", 3), ("f", 3),
]
ACT_ORDER = [
    ("masks", 0), ("xhi", 0), ("xhi", 1), ("x1hi", 0), ("xhi", 2), ("xhi", 3),
    ("hout", 0), ("qkhi", 0), ("gatet", 0), ("qkhi", 1), ("x1hi", 1), ("pqw", 0), ("wout", 0), ("hout", 1), ("qkhi", 2),
    ("qkhi", 3), ("gatet", 1), ("x1hi", 2), ("hout", 2), ("pqw", 1), ("wout", 1), ("elu", 0), ("qkhi", 4), ("qkhi", 5),
    ("vout", 0), ("x1hi", 3), ("vout", 1), ("exp", 0), ("gatet", 2), ("pqw", 2), ("wout", 2), ("hout", 3),
    ("exp", 1), ("chi", 0), ("elu", 1), ("vout", 2), ("pqw", 3), ("wout", 3), ("exp", 2), ("chi", 1),
    ("vout", 3), ("exp", 3), ("chi", 2), ("elu", 2), ("gatet", 3), ("chi", 3), ("elu", 3),
]
DVE_ORDER = [
    ("xlo", 0), ("xlo", 1), ("x1lo", 0), ("xlo", 2), ("xlo", 3),
    ("qklo", 0), ("sd", 0), ("qklo", 1), ("x1lo", 1), ("qklo", 2), ("e", 0), ("qklo", 3), ("sd", 1),
    ("x1lo", 2), ("scale1", 0), ("e", 1), ("qklo", 4), ("qklo", 5), ("sd", 2), ("max", 0), ("x1lo", 3), ("fin1", 0),
    ("max", 1), ("out1", 0), ("scale1", 1), ("norm0", 0), ("e", 2), ("clo", 0), ("sd", 3), ("max", 2), ("norm0", 1), ("y0", 0),
    ("fin1", 1), ("clo", 1), ("x1", 0), ("max", 3), ("norm0", 2), ("out1", 1), ("e", 3), ("y0", 1), ("clo", 2), ("scale1", 2),
    ("x1", 1), ("norm0", 3), ("y0", 2), ("mx", 0), ("mx", 1), ("clo", 3), ("scale1", 3), ("fin1", 2), ("x1", 2), ("y0", 3), ("out1", 2), ("fin1", 3),
    ("x1", 3), ("out1", 3),
]
POOL_ORDER = [
    ("xb", 0), ("prod", 0), ("prod", 1), ("fb", 0), ("prod", 2), ("rstd1", 0), ("fb", 1), ("prod", 3),
    ("rstd0", 0), ("rstd1", 1), ("rstd0", 1), ("fb", 2), ("rstd0", 2), ("fb", 3), ("rstd1", 2), ("rstd0", 3), ("rstd1", 3),
]
LAYER0 = {"xT", "qk", "s", "v", "st", "pv0", "cT", "f", "maskT", "masks", "xhi", "qkhi", "vout", "exp", "chi",
          "xlo", "qklo", "max", "norm0", "clo", "y0", "x1", "mx", "xb", "rstd0"}


def upto(group, per, k):
    return group * per + k


def bass_graph_transformer_gat(nc, x, adj, Wq, bq, Wk, bk, Wv, bv, Wf, bf, W1, b1, w_src, w_dst, H_w, H_b, out):
    graphs, nodes, D = x.shape
    NG = graphs // GROUP
    KT = D // P
    H0, HD0 = 6, 64
    H1, _, HD1 = W1.shape
    PAIRS = H0 // 2
    GN = GROUP * P
    SCALE = float(HD0) ** -0.5
    HI, LO = 0, 1
    THREE = ((HI, HI), (HI, LO), (LO, HI))
    assert nodes == P and KT * P == D and H0 * HD0 == D and H1 * HD1 == D

    with ExitStack() as ctx:
        def sb(name, shape, dt=F32):
            return ctx.enter_context(nc.sbuf_tensor(name, shape, dt))

        def psum(name, shape, dt=F32):
            return ctx.enter_context(nc.psum_tensor(name, shape, dt))

        def sem(name):
            return ctx.enter_context(nc.semaphore(name))

        t_bank = [psum(f"t_bank{i}", [P, 512]) for i in range(2)]
        p_bank = [psum(f"p_bank{i}", [P, 512]) for i in range(2)]
        scores = psum("scores", [P, 2, 512])
        context0 = psum("context0", [P, 512])
        context1 = psum("context1", [P, 512])

        names = ("q", "k", "v", "f", "h", "g")
        w = {n: sb(f"w_{n}", [P, 2, KT, D], F32R) for n in names}
        ident = sb("ident", [P, P])
        ident_r = sb("ident_r", [P, P], F32R)
        ident_b = sb("ident_b", [P, P], BF16)
        ones_b = sb("ones_b", [P, P], BF16)
        bias_q = sb("bias_q", [P, 2, PAIRS])
        bias_v = sb("bias_v", [P, KT])
        bias_f = sb("bias_f", [P, D])
        out_bias = sb("out_bias", [P, D])
        bias_1 = sb("bias_1", [P, HD1])
        w_sd = sb("w_sd", [P, 2, D])
        sd_shift = sb("sd_shift", [P, 2, H1])
        gate_bias = sb("gate_bias", [P, D])
        gate_bias_parts = sb("gate_bias_parts", [P, D], BF16)
        eps0 = sb("eps0", [P, 1])
        eps1 = sb("eps1", [P, 1])
        minus_half = sb("minus_half", [P, 1])

        x_in = sb("x_in", [P, GROUP, D])
        x_res = sb("x_res", [P, GROUP, D])
        adj_in = sb("adj_in", [P, GROUP, P], U8)
        adj_b = sb("adj_b", [P, GROUP, P], BF16)
        neg = sb("neg", [P, GROUP, P], BF16)
        xT = sb("xT", [P, 2, KT, GN], F32R)
        qT = sb("qT", [P, 2, PAIRS, GN], F32R)
        kT = sb("kT", [P, 2, PAIRS, GN], F32R)
        v = sb("v", [P, GROUP, H0, HD0 + 1])
        neg_max = sb("neg_max", [P, H0], F32R)
        probs0 = sb("probs0", [P, 2, 2, PAIRS * P])
        rden0 = sb("rden0", [P, H0])
        ctx0 = sb("ctx0", [P, D])
        cT = sb("cT", [P, 2, KT, P], F32R)
        sum0 = sb("sum0", [P, 2, D])
        stats0 = sb("stats0", [P, GROUP, 6])
        mv0 = sb("mv0", [P, GROUP, 2])
        ve0 = sb("ve0", [P, GROUP])
        rstd0 = sb("rstd0", [P, GROUP])
        x1 = sb("x1", [P, GROUP, D])
        clip = sb("clip", [P, GROUP, P])
        x1T = sb("x1T", [P, 2, KT, P], F32R)
        th = sb("th", [P, D])
        h = sb("h", [P, 2, H1, HD1 + 1])
        gate_t = sb("gate_t", [P, 2, D])
        prod = sb("prod", [P, 2, D])
        sd = sb("sd", [P, 2, H1])
        sda = sb("sda", [P, 2, H1])
        wlog = sb("wlog", [P, H1])
        pqw = sb("pqw", [P, 2, 3, H1])
        w_all = sb("w_all", [P, H1, P])
        weights = sb("weights", [P, H1, P])
        rden1 = sb("rden1", [P, H1])
        f_raw = sb("f_raw", [P, D])
        f_b = sb("f_b", [P, 2, D])
        f_neg = sb("f_neg", [P, D])
        f_exp = sb("f_exp", [P, D])
        mix = sb("mix", [P, D])
        sum1 = sb("sum1", [P, 2, D])
        stats1 = sb("stats1", [P, GROUP, 6])
        mv1 = sb("mv1", [P, GROUP, 2])
        ve1 = sb("ve1", [P, GROUP])
        rstd1 = sb("rstd1", [P, GROUP])
        y_out = sb("y_out", [P, 2, D])
        stage = {"q": w_all, "k": weights, "v": x_res, "f": probs0, "h": x1, "g": y_out}
        stage_ap = {
            "q": w_all[:].rearrange("p h i -> p (h i)")[:, 0:KT * D],
            "k": weights[:].rearrange("p h i -> p (h i)")[:, 0:KT * D],
            "v": x_res[:].rearrange("p g d -> p (g d)")[:, 0:KT * D],
            "f": probs0[:].rearrange("p a b c -> p (a b c)")[:, 0:KT * D],
            "h": x1[:].rearrange("p g d -> p (g d)")[:, 0:KT * D],
        }
        stage_g = sb("stage_g", [P, KT, D])
        stage_ap["g"] = stage_g[:].rearrange("p k n -> p (k n)")
        stage_ap = {n: a.rearrange("p (k n) -> p k n", k=KT) for n, a in stage_ap.items()}
        dmas = {n: sem(f"w_{n}_loaded") for n in names}

        s_const = sem("const_made")
        s_bias = sem("bias_loaded")
        s_whi = sem("w_hi_made")
        s_wlo = sem("w_lo_made")
        s_gT = sem("g_transposed")
        s_gTlo = sem("g_lo_made")
        s_ob = sem("out_bias_summed")
        s_prep = sem("prep_done")
        s_link = sem("prep_link")
        s_pool = sem("pool_prep")
        s_free = sem("inputs_free")
        s_x = sem("x_loaded")
        s_adj = sem("adj_loaded")
        s_store = [sem(f"stored{i}") for i in range(2)]
        pe = {n: sem(f"pe_{n}") for n in ("xT", "qk", "s", "v", "st", "pv0", "cT", "f", "maskT",
                                           "x1T", "h", "gate", "wb", "pv1")}
        s_neg = sem("neg_made")
        s_adjb = sem("adj_b_made")
        s_xhi = sem("x_hi_made")
        s_qkhi = sem("qk_hi_made")
        s_v = sem("v_copied")
        s_exp = sem("probs0_made")
        s_chi = sem("c_hi_made")
        s_x1hi = sem("x1_hi_made")
        s_th = sem("th_made")
        s_h = sem("h_copied")
        s_gate = sem("gate_made")
        s_pqw = sem("pqw_made")
        s_wall = sem("w_all_copied")
        s_fneg = sem("f_neg_made")
        s_elu = sem("f_exp_made")
        s_xlo = sem("x_lo_made")
        s_qklo = sem("qk_lo_made")
        s_max = sem("max_found")
        s_rden0 = sem("rden0_made")
        s_ctx0 = sem("ctx0_made")
        s_clo = sem("c_lo_made")
        s_sum0 = sem("sum0_made")
        s_st0 = sem("stats0_made")
        s_seen = sem("stats_seen")
        s_mv0 = sem("mv0_made")
        s_x1 = sem("x1_made")
        s_mx = sem("clip_made")
        s_x1lo = sem("x1_lo_made")
        s_sd = sem("sd_made")
        s_sda = sem("sd_shifted")
        s_wlog = sem("w_exponent_made")
        s_eraw = sem("weights_made")
        s_e = sem("weights_clipped")
        s_rden1 = sem("rden1_made")
        s_fraw = sem("f_made")
        s_mix = sem("mix_step")
        s_sum1 = sem("sum1_made")
        s_st1 = sem("stats1_made")
        s_mv1 = sem("mv1_made")
        s_y = sem("y_made")
        s_xb = sem("x_res_made")
        s_ve0 = sem("var_eps0_made")
        s_rstd0 = sem("rstd0_made")
        s_prod = sem("prod_made")
        s_fb = sem("f_b_made")
        s_ve1 = sem("var_eps1_made")
        s_rstd1 = sem("rstd1_made")

        x_dram = x.rearrange("g p d -> p g d")
        out_dram = out.rearrange("g p d -> p g d")
        adj_dram = adj.rearrange("g p m -> p g m")

        def wait(eng, s, n):
            if not isinstance(n, int) or n > 0:
                eng.wait_ge(s, n)

        def phases(eng, step, order):
            for name, k in order:
                if name in LAYER0:
                    step(name, k, 0, None)
            with eng.Fori(0, NG - 1) as u:
                for name, k in order:
                    step(name, k, u + 1, u)
            for name, k in order:
                if name not in LAYER0:
                    step(name, k, None, NG - 1)

        def heads0(ap):
            return ap.rearrange("p (b j) -> p b j", b=2)

        def over_heads(ap, n):
            return ap.unsqueeze(1).broadcast_to([P, n, ap.shape[-1]])

        def per_head(ap, n):
            return ap.unsqueeze(2).broadcast_to([P, ap.shape[-1], n])

        block = ctx.enter_context(nc.Block())

        @block.sync
        def _(sp):
            sp.dma_start(x_in[:], x_dram[:, 0:GROUP, :]).then_inc(s_x, 16)
            sp.dma_start(adj_in[:], adj_dram[:, 0:GROUP, :]).then_inc(s_adj, 16)
            for n, src in (("q", Wq), ("k", Wk), ("v", Wv), ("f", Wf), ("g", H_w)):
                sp.dma_start(stage_ap[n], src.rearrange("(k p) n -> p k n", p=P)).then_inc(dmas[n], 16)
            for kt in range(KT):
                sp.dma_start(stage_ap["h"][:, kt, :].rearrange("p (a e) -> p a e", a=H1),
                             W1[:, kt * P:(kt + 1) * P, :].rearrange("a p e -> p a e")).then_inc(dmas["h"], 16)

            def at(n):
                return n if isinstance(n, int) else sp.snap(n)

            def load(t):
                first = at(t * GROUP)
                sp.wait_ge(pe["xT"], upto(t, GROUP, 0))
                sp.wait_ge(s_xb, upto(t, 1, 0))
                sp.wait_ge(s_adjb, upto(t, 1, 0))
                sp.sem_inc(s_free, 1)
                sp.dma_start(x_in[:], x_dram[:, bass.ds(first, GROUP), :]).then_inc(s_x, 16)
                sp.dma_start(adj_in[:], adj_dram[:, bass.ds(first, GROUP), :]).then_inc(s_adj, 16)

            def store(t):
                for g in range(GROUP):
                    graph = at(t * GROUP + g)
                    sp.wait_ge(s_y, upto(t, GROUP, g + 1))
                    sp.dma_start(out_dram[:, bass.ds(graph, 1), :],
                                 y_out[:, g % 2, :].unsqueeze(1)).then_inc(s_store[g % 2], 16)

            load(1)
            with sp.Fori(0, NG - 2) as u:
                load(u + 2)
                store(u)
            store(NG - 2)
            store(NG - 1)
            for g in range(2):
                sp.wait_ge(s_store[g], graphs // 2 * 16)

        @block.tensor
        def _(te):
            te.wait_ge(s_const, 3)
            te.wait_ge(dmas["g"], 16)
            for kt in range(KT):
                if kt >= 2:
                    te.wait_ge(s_gTlo, kt - 1)
                for ot in range(KT):
                    last = te.transpose(t_bank[kt % 2][:, ot * P:(ot + 1) * P],
                                        stage_ap["g"][:, ot, kt * P:(kt + 1) * P], ident[:])
                last.then_inc(s_gT, 1)
            te.wait_ge(s_bias, 7 * 16)
            te.wait_ge(dmas["f"], 16)
            for kt in range(KT):
                last = te.matmul(p_bank[0][:, 0:D], bias_v[:, kt:kt + 1].broadcast_to([P, P]),
                                 stage_ap["f"][:, kt, :], start=(kt == 0), stop=(kt == KT - 1))
            last.then_inc(s_ob, 1)
            te.wait_ge(s_prep, 1)

            t_freed = {"xT": (s_xlo, GROUP), "x1T": (s_x1lo, GROUP), "cT": (s_clo, GROUP),
                       "wb": (s_wall, 3 * GROUP), "maskT": (s_mx, 2)}
            p_freed = {"qk": (s_qklo, 2 * PAIRS), "v": (s_v, GROUP), "f": (s_sum0, GROUP),
                       "h": (s_h, GROUP), "gate": (s_gate, GROUP)}

            def uses(freed, phase):
                found = []
                for name, k in PE_ORDER:
                    if name in freed and phase != ("last" if name in LAYER0 else "first"):
                        found += [(name, 3 * k + r) for r in range(3)] if name == "wb" else [(name, k)]
                return found

            def bank(banks, freed, name, k, g0, g1):
                order = uses(freed, "first" if g1 is None else "last" if g0 is None else "loop")
                at = order.index((name, k))
                if at >= 2:
                    before, kb = order[at - 2]
                    s, per = freed[before]
                    te.wait_ge(s, upto(g0 if before in LAYER0 else g1, per, kb + 1))
                elif g1 is not None:
                    before, kb = uses(freed, "loop")[at - 2]
                    assert before in LAYER0
                    s, per = freed[before]
                    te.wait_ge(s, upto(g1, per, kb + 1))
                return banks[at % 2]

            def project(dst, left, right, opened=False):
                n = 0
                for kt in range(KT):
                    for a, b in THREE:
                        last = te.matmul(dst, left(a, kt), right(b, kt), start=(n == 0 and not opened),
                                         stop=(n == 3 * KT - 1))
                        n += 1
                return last

            def head(ap, part, j, b, g):
                return ap[b * HD0:(b + 1) * HD0, part, j, g * P:(g + 1) * P]

            def step(name, k, g0, g1):
                if name == "xT":
                    if k == 0:
                        te.wait_ge(s_x, upto(g0, 16, 16))
                    dst = bank(t_bank, t_freed, name, k, g0, g1)
                    for kt in range(KT):
                        last = te.transpose(dst[:, kt * P:(kt + 1) * P], x_in[:, k, kt * P:(kt + 1) * P], ident[:])
                    last.then_inc(pe["xT"], 1)
                elif name == "qk":
                    if k == 0:
                        te.wait_ge(s_xlo, upto(g0, GROUP, GROUP))
                    dst = bank(p_bank, p_freed, name, k, g0, g1)
                    j, m = k // 2, w["qk"[k % 2]]
                    project(dst[:, :], lambda a, kt: m[:, a, kt, j * P:(j + 1) * P],
                            lambda b, kt: xT[:, b, kt, :]).then_inc(pe["qk"], 1)
                elif name == "v":
                    dst = bank(p_bank, p_freed, name, k, g0, g1)
                    project(dst[:, 0:D], lambda a, kt: xT[:, a, kt, k * P:(k + 1) * P],
                            lambda b, kt: w["v"][:, b, kt, :]).then_inc(pe["v"], 1)
                elif name == "s":
                    if k == 0:
                        te.wait_ge(s_qklo, upto(g0, 2 * PAIRS, 2 * PAIRS))
                        te.wait_ge(s_neg, upto(g0, 1, 1))
                    wait(te, s_exp, upto(g0, GROUP, k))
                    for b in range(2):
                        te.matmul(scores[:, b, 0:PAIRS * P], ident_b[:], over_heads(neg[:, k, :], PAIRS),
                                  start=True, stop=False)
                    for j in range(PAIRS):
                        for b in range(2):
                            last = te.matmul(scores[:, b, j * P:(j + 1) * P], head(qT, HI, j, b, k),
                                             head(kT, HI, j, b, k), start=False, stop=(j == PAIRS - 1))
                    last.then_inc(pe["s"], 1)
                elif name == "st":
                    te.wait_ge(s_max, upto(g0, GROUP, k + 1))
                    for b in range(2):
                        te.matmul(scores[:, b, 0:PAIRS * P], neg[:, k, :], over_heads(ident_b[:], PAIRS),
                                  start=True, stop=False)
                    for a, c in THREE:
                        for j in range(PAIRS):
                            for b in range(2):
                                te.matmul(scores[:, b, j * P:(j + 1) * P], head(kT, a, j, b, k),
                                          head(qT, c, j, b, k), start=False, stop=False)
                    for b in range(2):
                        for j in range(PAIRS):
                            n = b * PAIRS + j
                            last = te.matmul(scores[:, b, j * P:(j + 1) * P],
                                             neg_max[:, n:n + 1].broadcast_to([P, P]), ident_r[:],
                                             start=False, stop=(j == PAIRS - 1))
                    last.then_inc(pe["st"], 1)
                elif name == "pv0":
                    te.wait_ge(s_exp, upto(g0, GROUP, k + 1))
                    te.wait_ge(s_v, upto(g0, GROUP, k + 1))
                    wait(te, s_ctx0, upto(g0, GROUP, k))
                    for j in range(PAIRS):
                        for b in range(2):
                            n = 2 * j + b
                            last = te.matmul(context0[:, n * (HD0 + 1):(n + 1) * (HD0 + 1)],
                                             probs0[:, k % 2, b, j * P:(j + 1) * P], v[:, k, n, :],
                                             start=True, stop=True)
                    last.then_inc(pe["pv0"], 1)
                elif name == "cT":
                    te.wait_ge(s_ctx0, upto(g0, GROUP, k + 1))
                    dst = bank(t_bank, t_freed, name, k, g0, g1)
                    for kt in range(KT):
                        last = te.transpose(dst[:, kt * P:(kt + 1) * P], ctx0[:, kt * P:(kt + 1) * P], ident[:])
                    last.then_inc(pe["cT"], 1)
                elif name == "f":
                    te.wait_ge(s_clo, upto(g0, GROUP, k + 1))
                    dst = bank(p_bank, p_freed, name, k, g0, g1)
                    project(dst[:, 0:D], lambda a, kt: cT[:, a, kt, :],
                            lambda b, kt: w["f"][:, b, kt, :]).then_inc(pe["f"], 1)
                elif name == "maskT":
                    dst = bank(t_bank, t_freed, name, k, g0, g1)
                    if k == 0:
                        te.wait_ge(s_adjb, upto(g0, 1, 1))
                    for i in range(2):
                        last = te.transpose(dst[:, 0:P].bitcast(BF16)[:, i * P:(i + 1) * P],
                                            adj_b[:, 2 * k + i, :], ident_b[:])
                    last.then_inc(pe["maskT"], 1)
                elif name == "x1T":
                    te.wait_ge(s_x1, upto(g1, GROUP, k + 1))
                    dst = bank(t_bank, t_freed, name, k, g0, g1)
                    for kt in range(KT):
                        last = te.transpose(dst[:, kt * P:(kt + 1) * P], x1[:, k, kt * P:(kt + 1) * P], ident[:])
                    last.then_inc(pe["x1T"], 1)
                elif name == "h":
                    te.wait_ge(s_x1lo, upto(g1, GROUP, k + 1))
                    dst = bank(p_bank, p_freed, name, k, g0, g1)
                    project(dst[:, 0:D], lambda a, kt: x1T[:, a, kt, :],
                            lambda b, kt: w["h"][:, b, kt, :]).then_inc(pe["h"], 1)
                elif name == "gate":
                    dst = bank(p_bank, p_freed, name, k, g0, g1)
                    te.matmul(dst[:, 0:D], ones_b[:], gate_bias_parts[:], start=True, stop=False)
                    project(dst[:, 0:D], lambda a, kt: x1T[:, a, kt, :],
                            lambda b, kt: w["g"][:, b, kt, :], opened=True).then_inc(pe["gate"], 1)
                elif name == "wb":
                    te.wait_ge(s_pqw, upto(g1, 3 * GROUP, 3 * k + 3))
                    for r in range(3):
                        dst = bank(t_bank, t_freed, name, 3 * k + r, g0, g1)
                        for i in range(4):
                            n = 4 * r + i
                            last = te.transpose(dst[:, i * P:(i + 1) * P],
                                                pqw[:, k % 2, 2, n:n + 1].broadcast_to([P, P]), ident[:])
                        last.then_inc(pe["wb"], 1)
                elif name == "pv1":
                    te.wait_ge(s_e, upto(g1, GROUP, k + 1))
                    te.wait_ge(s_h, upto(g1, GROUP, k + 1))
                    wait(te, s_fraw, upto(g1, GROUP, k))
                    for n in range(H1):
                        last = te.matmul(context1[:, n * (HD1 + 1):(n + 1) * (HD1 + 1)], weights[:, n, :],
                                         h[:, k % 2, n, :], start=True, stop=True)
                    last.then_inc(pe["pv1"], 1)

            phases(te, step, PE_ORDER)

        @block.scalar
        def _(act):
            for n, src in ((0, bq), (1, bk)):
                act.dma_start(bias_q[:, n, :], src.rearrange("(m p) -> p m", p=P), allow_slow_non_contiguous=True).then_inc(s_bias, 16)
            act.dma_start(bias_v[:], bv.rearrange("(m p) -> p m", p=P), allow_slow_non_contiguous=True).then_inc(s_bias, 16)
            act.dma_start(bias_f[:], bf.partition_broadcast(P)).then_inc(s_bias, 16)
            act.dma_start(bias_1[:], b1.partition_broadcast(P)).then_inc(s_bias, 16)
            act.dma_start(w_sd[:, 0, :], w_src.rearrange("a e o -> (a e o)").partition_broadcast(P)).then_inc(s_bias, 16)
            act.dma_start(gate_bias[:], H_b.partition_broadcast(P)).then_inc(s_bias, 16)
            act.dma_start(w_sd[:, 1, :], w_dst.rearrange("a e o -> (a e o)").partition_broadcast(P)).then_inc(s_bias, 16)
            act.wait_ge(s_const, 4)
            act.activation(ident_b[:], ident[:], ACT.Copy).then_inc(s_link, 1)
            act.activation(ident_r[:], ident[:], ACT.Copy).then_inc(s_link, 1)
            act.activation(ve0[:, 0:1], eps0[:], ACT.Exp).then_inc(s_link, 1)
            for n in ("q", "k", "v", "h", "f"):
                act.wait_ge(dmas[n], 16 * KT if n == "h" else 16)
                act.activation(w[n][:, HI], stage_ap[n], ACT.Copy).then_inc(s_whi, 1)
            for kt in range(KT):
                act.wait_ge(s_gT, kt + 1)
                act.activation(w["g"][:, HI, kt, :], t_bank[kt % 2][:, 0:D], ACT.Copy).then_inc(s_whi, 1)
            act.wait_ge(s_prep, 1)

            def step(name, k, g0, g1):
                if name == "masks":
                    act.wait_ge(s_adj, upto(g0, 16, 16))
                    wait(act, pe["st"], upto(g0, GROUP, 0))
                    act.activation(neg[:], adj_in[:], ACT.Copy, scale=-MASKED, bias=MASKED).then_inc(s_neg, 1)
                    wait(act, pe["maskT"], upto(g0, 2, 0))
                    act.activation(adj_b[:], adj_in[:], ACT.Copy).then_inc(s_adjb, 1)
                elif name == "xhi":
                    act.wait_ge(pe["xT"], upto(g0, GROUP, k + 1))
                    if k == 0:
                        wait(act, pe["v"], upto(g0, GROUP, 0))
                    act.activation(xT[:, HI, :, k * P:(k + 1) * P],
                                   t_bank[t_at("xT", k, g1)][:, 0:D].rearrange("p (k n) -> p k n", k=KT),
                                   ACT.Copy).then_inc(s_xhi, 1)
                elif name == "qkhi":
                    act.wait_ge(pe["qk"], upto(g0, 2 * PAIRS, k + 1))
                    if k == 0:
                        wait(act, pe["st"], upto(g0, GROUP, 0))
                    dst = (qT, kT)[k % 2]
                    act.activation(dst[:, HI, k // 2, :], p_bank[p_at("qk", k, g1)][:, :], ACT.Identity,
                                   bias=bias_q[:, k % 2, k // 2:k // 2 + 1]).then_inc(s_qkhi, 1)
                elif name == "vout":
                    act.wait_ge(pe["v"], upto(g0, GROUP, k + 1))
                    wait(act, pe["pv0"], upto(g0, GROUP, k + 1 - GROUP))
                    act.activation(v[:, k, :, 0:HD0],
                                   p_bank[p_at("v", k, g1)][:, 0:D].rearrange("p (h e) -> p h e", h=H0),
                                   ACT.Copy).then_inc(s_v, 1)
                elif name == "exp":
                    act.wait_ge(pe["st"], upto(g0, GROUP, k + 1))
                    wait(act, pe["pv0"], upto(g0, GROUP, k - 1))
                    act.activation(probs0[:, k % 2], scores[:, :, 0:PAIRS * P], ACT.Exp,
                                   scale=SCALE).then_inc(s_exp, 1)
                elif name == "chi":
                    act.wait_ge(pe["cT"], upto(g0, GROUP, k + 1))
                    wait(act, pe["f"], upto(g0, GROUP, k))
                    act.activation(cT[:, HI], t_bank[t_at("cT", k, g1)][:, 0:D].rearrange("p (k n) -> p k n", k=KT),
                                   ACT.Copy).then_inc(s_chi, 1)
                elif name == "x1hi":
                    act.wait_ge(pe["x1T"], upto(g1, GROUP, k + 1))
                    wait(act, pe["gate"], upto(g1, GROUP, k))
                    act.activation(x1T[:, HI], t_bank[t_at("x1T", k, g1, g0)][:, 0:D].rearrange("p (k n) -> p k n", k=KT),
                                   ACT.Copy).then_inc(s_x1hi, 1)
                elif name == "hout":
                    src = p_bank[p_at("h", k, g1, g0)][:, 0:D]
                    act.wait_ge(pe["h"], upto(g1, GROUP, k + 1))
                    wait(act, s_prod, upto(g1, GROUP, k))
                    act.activation(th[:], src, ACT.Tanh).then_inc(s_th, 1)
                    wait(act, pe["pv1"], upto(g1, GROUP, max(k - 1, 0)))
                    act.activation(h[:, k % 2, :, 0:HD1], src.rearrange("p (h e) -> p h e", h=H1),
                                   ACT.Copy).then_inc(s_h, 1)
                elif name == "gatet":
                    act.wait_ge(pe["gate"], upto(g1, GROUP, k + 1))
                    wait(act, s_sum1, upto(g1, GROUP, max(k - 1, 0)))
                    act.activation(gate_t[:, k % 2, :], p_bank[p_at("gate", k, g1, g0)][:, 0:D], ACT.Tanh,
                                   scale=0.5).then_inc(s_gate, 1)
                elif name == "pqw":
                    act.wait_ge(s_sda, upto(g1, GROUP, k + 1))
                    wait(act, s_eraw, upto(g1, GROUP, max(k - 1, 0)))
                    act.activation(pqw[:, k % 2, 0, :], sda[:, 1, :], ACT.Exp).then_inc(s_pqw, 1)
                    act.activation(pqw[:, k % 2, 1, :], sda[:, 1, :], ACT.Exp, scale=LEAKY).then_inc(s_pqw, 1)
                    act.wait_ge(s_wlog, upto(g1, GROUP, k + 1))
                    wait(act, pe["wb"], upto(g1, 3 * GROUP, 3 * max(k - 1, 0)))
                    act.activation(pqw[:, k % 2, 2, :], wlog[:], ACT.Exp, scale=LEAKY - 1.0).then_inc(s_pqw, 1)
                elif name == "wout":
                    wait(act, s_eraw, upto(g1, GROUP, k))
                    for r in range(3):
                        act.wait_ge(pe["wb"], upto(g1, 3 * GROUP, 3 * k + r + 1))
                        act.activation(w_all[:, 4 * r:4 * r + 4, :],
                                       t_bank[t_at("wb", 3 * k + r, g1, g0)][:, :].rearrange("p (h i) -> p h i", h=4),
                                       ACT.Copy).then_inc(s_wall, 1)
                elif name == "elu":
                    wait(act, s_elu, upto(g1, GROUP, k))
                    act.wait_ge(s_fb, upto(g1, GROUP, k + 1))
                    act.activation(f_neg[:], f_b[:, k % 2, :], ACT.Relu, scale=-1.0).then_inc(s_fneg, 1)
                    act.wait_ge(s_fneg, upto(g1, GROUP, k + 1))
                    wait(act, s_mix, upto(g1, 3 * GROUP, 3 * k))
                    act.activation(f_exp[:], f_neg[:], ACT.Exp, scale=-1.0).then_inc(s_elu, 1)

            phases(act, step, ACT_ORDER)

        @block.vector
        def _(dve):
            linked = [0]

            def link(ins):
                linked[0] += 1
                ins.then_inc(s_pool, 1)
                dve.wait_ge(s_pool, linked[0])

            dve.memset(v[:, :, :, HD0:HD0 + 1], 1.0)
            dve.memset(h[:, :, :, HD1:HD1 + 1], 1.0)
            dve.memset(eps1[:], LN_EPS / 4)
            link(dve.memset(gate_bias_parts[:], 0.0))
            dve.wait_ge(s_bias, 8 * 16)
            rest = mix
            link(dve.tensor_copy(gate_bias_parts[0:1, :], gate_bias[0:1, :]))
            part = prod[:].rearrange("p a d -> p (a d)").bitcast(BF16)[:, 0:D]
            link(dve.tensor_copy(part, gate_bias[:]))
            link(dve.tensor_tensor(rest[:], gate_bias[:], part, ALU.subtract))
            link(dve.tensor_copy(gate_bias_parts[32:33, :], rest[32:33, :]))
            link(dve.tensor_copy(part, rest[:]))
            link(dve.tensor_tensor(rest[:], rest[:], part, ALU.subtract))
            link(dve.tensor_copy(gate_bias_parts[64:65, :], rest[64:65, :]))
            link(dve.tensor_reduce(sd_shift[:, 0, :], w_sd[:, 1, :].rearrange("p (h e) -> p h e", h=H1), AX_X,
                                   ALU.add, apply_absolute_value=True))
            link(dve.tensor_scalar(sd_shift[:, 0, :], sd_shift[:, 0, :], -EXP_ROOM, 0.0, ALU.add, ALU.max))
            link(dve.tensor_scalar(sd_shift[:, 1, :], sd_shift[:, 0, :], -1.0, None, ALU.mult))
            for i, n in enumerate(("q", "k", "v", "h", "f")):
                dve.wait_ge(s_whi, i + 1)
                dve.tensor_tensor(w[n][:, LO], stage_ap[n], w[n][:, HI].bitcast(F32), ALU.subtract).then_inc(s_wlo, 1)
            for kt in range(KT):
                dve.wait_ge(s_whi, 6 + kt)
                dve.tensor_tensor(w["g"][:, LO, kt, :], t_bank[kt % 2][:, 0:D], w["g"][:, HI, kt, :].bitcast(F32),
                                  ALU.subtract).then_inc(s_gTlo, 1)
            dve.wait_ge(s_ob, 1)
            link(dve.tensor_tensor(out_bias[:], p_bank[0][:, 0:D], bias_f[:], ALU.add))
            dve.wait_ge(s_wlo, 5)
            dve.wait_ge(s_gTlo, KT)
            dve.wait_ge(s_link, 3)
            dve.memset(ve1[:], 0.0).then_inc(s_prep, 1)

            def low(dst, src, hi):
                return dve.tensor_tensor(dst, src, hi.bitcast(F32), ALU.subtract)

            def moments(y, stats, mv, made_y, made_stats, made_mv, n):
                dve.wait_ge(made_y, n)
                dve.bn_stats(stats, y).then_inc(made_stats, 1)
                dve.wait_ge(made_stats, n)
                dve.sem_inc(s_seen, 1)
                dve.bn_aggr(mv, stats).then_inc(made_mv, 1)

            def step(name, k, g0, g1):
                if name == "xlo":
                    dve.wait_ge(s_xhi, upto(g0, GROUP, k + 1))
                    cols = slice(k * P, (k + 1) * P)
                    low(xT[:, LO, :, cols], t_bank[t_at("xT", k, g1)][:, 0:D].rearrange("p (k n) -> p k n", k=KT),
                        xT[:, HI, :, cols]).then_inc(s_xlo, 1)
                elif name == "qklo":
                    dve.wait_ge(s_qkhi, upto(g0, 2 * PAIRS, k + 1))
                    dst = (qT, kT)[k % 2]
                    dve.scalar_tensor_tensor(out=dst[:, LO, k // 2, :], in0=p_bank[p_at("qk", k, g1)][:, :],
                                             scalar=bias_q[:, k % 2, k // 2:k // 2 + 1],
                                             in1=dst[:, HI, k // 2, :].bitcast(F32),
                                             op0=ALU.add, op1=ALU.subtract).then_inc(s_qklo, 1)
                elif name == "max":
                    dve.wait_ge(pe["s"], upto(g0, GROUP, k + 1))
                    wait(dve, pe["st"], upto(g0, GROUP, k))
                    dve.tensor_reduce(heads0(neg_max[:]),
                                      scores[:, :, 0:PAIRS * P].rearrange("p b (j n) -> p b j n", j=PAIRS),
                                      AX_X, ALU.max, negate=True).then_inc(s_max, 1)
                elif name == "norm0":
                    dve.wait_ge(pe["pv0"], upto(g0, GROUP, k + 1))
                    sums = context0[:, 0:H0 * (HD0 + 1)].rearrange("p (h e) -> p h e", h=H0)
                    dve.reciprocal(rden0[:], sums[:, :, HD0:HD0 + 1].rearrange("p h o -> p (h o)")).then_inc(s_rden0, 1)
                    dve.wait_ge(s_rden0, upto(g0, GROUP, k + 1))
                    wait(dve, pe["cT"], upto(g0, GROUP, k))
                    dve.tensor_tensor(ctx0[:].rearrange("p (h e) -> p h e", h=H0), sums[:, :, 0:HD0],
                                      per_head(rden0[:], HD0), ALU.mult).then_inc(s_ctx0, 1)
                elif name == "clo":
                    dve.wait_ge(s_chi, upto(g0, GROUP, k + 1))
                    low(cT[:, LO], t_bank[t_at("cT", k, g1)][:, 0:D].rearrange("p (k n) -> p k n", k=KT),
                        cT[:, HI]).then_inc(s_clo, 1)
                elif name == "y0":
                    dve.wait_ge(pe["f"], upto(g0, GROUP, k + 1))
                    if k == 0:
                        dve.wait_ge(s_xb, upto(g0, 1, 1))
                    wait(dve, s_x1, upto(g0, GROUP, k - 1))
                    dve.tensor_tensor(sum0[:, k % 2, :], p_bank[p_at("f", k, g1)][:, 0:D], x_res[:, k, :],
                                      ALU.add).then_inc(s_sum0, 1)
                    moments(sum0[:, k % 2, :], stats0[:, k, :], mv0[:, k, :], s_sum0, s_st0, s_mv0,
                            upto(g0, GROUP, k + 1))
                elif name == "x1":
                    dve.wait_ge(s_rstd0, upto(g0, GROUP, k + 1))
                    if g1 is not None:
                        dve.wait_ge(s_sum1, upto(g1, GROUP, k + 1))
                    dve.tensor_scalar(x1[:, k, :], sum0[:, k % 2, :], mv0[:, k, 0:1], rstd0[:, k:k + 1],
                                      ALU.subtract, ALU.mult).then_inc(s_x1, 1)
                elif name == "mx":
                    dve.wait_ge(pe["maskT"], upto(g0, 2, k + 1))
                    if g1 is not None:
                        dve.wait_ge(s_e, upto(g1, GROUP, GROUP))
                    src = t_bank[t_at("maskT", k, g1)][:, 0:P].bitcast(BF16).rearrange("p (i n) -> p i n", i=2)
                    dve.tensor_scalar(clip[:, 2 * k:2 * k + 2, :], src, KEEP, FLOOR, ALU.mult, ALU.add).then_inc(s_mx, 1)
                elif name == "x1lo":
                    dve.wait_ge(s_x1hi, upto(g1, GROUP, k + 1))
                    low(x1T[:, LO], t_bank[t_at("x1T", k, g1, g0)][:, 0:D].rearrange("p (k n) -> p k n", k=KT),
                        x1T[:, HI]).then_inc(s_x1lo, 1)
                elif name == "sd":
                    dve.wait_ge(s_prod, upto(g1, GROUP, k + 1))
                    dve.tensor_reduce(sd[:].rearrange("p a h -> p (a h)"),
                                      prod[:].rearrange("p a (h e) -> p (a h) e", h=H1), AX_X,
                                      ALU.add).then_inc(s_sd, 1)
                    dve.wait_ge(s_sd, upto(g1, GROUP, k + 1))
                    wait(dve, s_pqw, upto(g1, 3 * GROUP, 3 * k))
                    dve.tensor_tensor(sda[:], sd[:], sd_shift[:], ALU.add).then_inc(s_sda, 1)
                    dve.wait_ge(s_sda, upto(g1, GROUP, k + 1))
                    dve.tensor_scalar(wlog[:], sda[:, 0, :], -EXP_ROOM, None, ALU.max).then_inc(s_wlog, 1)
                elif name == "e":
                    dve.wait_ge(s_wall, upto(g1, 3 * GROUP, 3 * k + 3))
                    wait(dve, pe["pv1"], upto(g1, GROUP, k))
                    for n in range(H1):
                        last = dve.tensor_scalar(weights[:, n, :], w_all[:, n, :], pqw[:, k % 2, 1, n:n + 1],
                                                 pqw[:, k % 2, 0, n:n + 1], ALU.mult, ALU.max)
                    last.then_inc(s_eraw, 1)
                    dve.wait_ge(s_eraw, upto(g1, GROUP, k + 1))
                    dve.tensor_tensor(weights[:], weights[:], over_heads(clip[:, k, :], H1), ALU.min).then_inc(s_e, 1)
                elif name == "scale1":
                    dve.wait_ge(pe["pv1"], upto(g1, GROUP, k + 1))
                    sums = context1[:, 0:H1 * (HD1 + 1)].rearrange("p (h e) -> p h e", h=H1)
                    dve.reciprocal(rden1[:], sums[:, :, HD1:HD1 + 1].rearrange("p h o -> p (h o)")).then_inc(s_rden1, 1)
                    dve.wait_ge(s_rden1, upto(g1, GROUP, k + 1))
                    wait(dve, s_fb, upto(g1, GROUP, k))
                    dve.tensor_tensor(f_raw[:].rearrange("p (h e) -> p h e", h=H1), sums[:, :, 0:HD1],
                                      per_head(rden1[:], HD1), ALU.mult).then_inc(s_fraw, 1)
                elif name == "fin1":
                    dve.wait_ge(s_elu, upto(g1, GROUP, k + 1))
                    dve.scalar_tensor_tensor(out=mix[:], in0=f_b[:, k % 2, :], scalar=0.0, in1=f_exp[:],
                                             op0=ALU.max, op1=ALU.add).then_inc(s_mix, 1)
                    dve.wait_ge(s_mix, upto(g1, 3 * GROUP, 3 * k + 1))
                    dve.scalar_tensor_tensor(out=mix[:], in0=mix[:], scalar=-1.0, in1=x1[:, k, :],
                                             op0=ALU.add, op1=ALU.subtract).then_inc(s_mix, 1)
                    dve.wait_ge(s_mix, upto(g1, 3 * GROUP, 3 * k + 2))
                    dve.wait_ge(s_gate, upto(g1, GROUP, k + 1))
                    dve.scalar_tensor_tensor(out=mix[:], in0=gate_t[:, k % 2, :], scalar=1.0, in1=mix[:],
                                             op0=ALU.add, op1=ALU.mult).then_inc(s_mix, 1)
                    dve.wait_ge(s_mix, upto(g1, 3 * GROUP, 3 * k + 3))
                    wait(dve, s_y, upto(g1, GROUP, max(k - 1, 0)))
                    dve.scalar_tensor_tensor(out=sum1[:, k % 2, :], in0=mix[:], scalar=0.25, in1=x1[:, k, :],
                                             op0=ALU.mult, op1=ALU.add).then_inc(s_sum1, 1)
                    moments(sum1[:, k % 2, :], stats1[:, k, :], mv1[:, k, :], s_sum1, s_st1, s_mv1,
                            upto(g1, GROUP, k + 1))
                elif name == "out1":
                    dve.wait_ge(s_rstd1, upto(g1, GROUP, k + 1))
                    wait(dve, s_store[k % 2], upto(g1, GROUP // 2 * 16, k // 2 * 16))
                    dve.tensor_scalar(y_out[:, k % 2, :], sum1[:, k % 2, :], mv1[:, k, 0:1], rstd1[:, k:k + 1],
                                      ALU.subtract, ALU.mult).then_inc(s_y, 1)

            phases(dve, step, DVE_ORDER)

        @block.gpsimd
        def _(pool):
            pool.memset(ident[:], 0.0).then_inc(s_const, 1)
            pool.memset(ones_b[:], 1.0).then_inc(s_const, 1)
            pool.memset(eps0[:], LN_EPS)
            pool.wait_ge(s_const, 2)
            pool.affine_select(out=ident[:], in_=ident[:], compare_op=ALU.not_equal, fill=1.0, base=0,
                               pattern=[[-1, P]], channel_multiplier=1).then_inc(s_const, 1)
            pool.memset(minus_half[:], -0.5).then_inc(s_const, 1)
            pool.wait_ge(s_prep, 1)

            def rsqrt(mv, ve, rstd, eps, made_mv, made_ve, made_rstd, n):
                pool.wait_ge(made_mv, n)
                pool.tensor_tensor(ve, mv, eps[:], ALU.add).then_inc(made_ve, 1)
                pool.wait_ge(made_ve, n)
                pool.tensor_tensor(rstd, ve, minus_half[:], ALU.pow).then_inc(made_rstd, 1)

            def step(name, k, g0, g1):
                if name == "xb":
                    pool.wait_ge(s_x, upto(g0, 16, 16))
                    wait(pool, s_sum0, upto(g0, GROUP, 0))
                    pool.tensor_tensor(x_res[:], x_in[:], over_heads(out_bias[:], GROUP), ALU.add).then_inc(s_xb, 1)
                elif name == "rstd0":
                    rsqrt(mv0[:, k, 1:2], ve0[:, k:k + 1], rstd0[:, k:k + 1], eps0, s_mv0, s_ve0, s_rstd0,
                          upto(g0, GROUP, k + 1))
                elif name == "prod":
                    pool.wait_ge(s_th, upto(g1, GROUP, k + 1))
                    wait(pool, s_sd, upto(g1, GROUP, k))
                    pool.tensor_tensor(prod[:], over_heads(th[:], 2), w_sd[:], ALU.mult).then_inc(s_prod, 1)
                elif name == "fb":
                    pool.wait_ge(s_fraw, upto(g1, GROUP, k + 1))
                    wait(pool, s_mix, upto(g1, 3 * GROUP, max(3 * (k - 1), 0)))
                    pool.tensor_tensor(f_b[:, k % 2, :].rearrange("p (h e) -> p h e", h=H1),
                                       f_raw[:].rearrange("p (h e) -> p h e", h=H1),
                                       over_heads(bias_1[:], H1), ALU.add).then_inc(s_fb, 1)
                elif name == "rstd1":
                    rsqrt(mv1[:, k, 1:2], ve1[:, k:k + 1], rstd1[:, k:k + 1], eps1, s_mv1, s_ve1, s_rstd1,
                          upto(g1, GROUP, k + 1))

            phases(pool, step, POOL_ORDER)


T_STAGES = {"xT", "x1T", "cT", "wb", "maskT"}
P_STAGES = {"qk", "v", "f", "h", "gate"}


def bank_of(stages, name, k, first, last):
    found = []
    for n, i in PE_ORDER:
        if n in stages and not (first and n not in LAYER0) and not (last and n in LAYER0):
            found += [(n, 3 * i + r) for r in range(3)] if n == "wb" else [(n, i)]
    return found.index((name, k)) % 2


def t_at(name, k, g1, g0=0):
    return bank_of(T_STAGES, name, k, g1 is None, g0 is None)


def p_at(name, k, g1, g0=0):
    return bank_of(P_STAGES, name, k, g1 is None, g0 is None)


_INS = ['x', 'adj', 'L0_gnn_Wq', 'L0_gnn_bq', 'L0_gnn_Wk', 'L0_gnn_bk', 'L0_gnn_Wv', 'L0_gnn_bv', 'L0_gnn_Wf',
        'L0_gnn_bf', 'L1_gnn_W', 'L1_gnn_b', 'L1_gnn_w_src', 'L1_gnn_w_dst', 'L1_gnn_H_w', 'L1_gnn_H_b']
_OUTS = [((64, 128, 384), 'float32')]


def kernel(**inputs):
    import numpy as _np
    import concourse.bacc as _bacc
    from concourse import mybir as _mybir
    from concourse.bass_utils import run_bass_kernel_spmd as _run

    nc = _bacc.Bacc("TRN2", target_bir_lowering=False, num_devices=1)
    arrays, args = {}, []
    for name in _INS:
        a = _np.ascontiguousarray(inputs[name])
        arrays[f"in_{name}_dram"] = a
        args.append(nc.dram_tensor(f"in_{name}_dram", a.shape, _mybir.dt.from_np(a.dtype), kind="ExternalInput").ap())
    for i, (shape, dtype) in enumerate(_OUTS):
        dt = _mybir.dt.from_np(_np.dtype(dtype))
        args.append(nc.dram_tensor(f"out_{i}_dram", shape, dt, kind="ExternalOutput").ap())
    bass_graph_transformer_gat(nc, *args)
    r = _run(nc, [arrays], core_ids=[0])
    got = tuple(r.results[0][f"out_{i}_dram"] for i in range(len(_OUTS)))
    return got[0]
```

```python
from contextlib import ExitStack

import concourse.bass as bass
from concourse import mybir

F32 = mybir.dt.float32
F32R = mybir.dt.float32r
BF16 = mybir.dt.bfloat16
U8 = mybir.dt.uint8
ALU = mybir.AluOpType
ACT = mybir.ActivationFunctionType
AX_X = mybir.AxisListType.X

P = 128
GROUP = 4
MASKED = -(2.0 ** 56)
LN_EPS = 1e-5
LEAKY = 0.2
EXP_ROOM = 80.0
KEEP, FLOOR = 1e37, 1e-30

PE_ORDER = [
    ("x1T", 0), ("xT", 0), ("xT", 1), ("h", 0), ("xT", 2), ("xT", 3), ("gate", 0), ("x1T", 1), ("qk", 0), ("qk",
    1), ("h", 1), ("wb", 0), ("gate", 1), ("wb", 1), ("wb", 2), ("qk", 2), ("pv1", 0), ("pv1", 1), ("x1T", 2),
    ("pv1", 2), ("qk", 3), ("wb", 3), ("h", 2), ("qk", 4), ("qk", 5), ("wb", 4), ("v", 0), ("s", 0), ("gate",
    2), ("st", 0), ("stm", 0), ("pv1", 3), ("x1T", 3), ("wb", 5), ("s", 1), ("v", 1), ("pv0", 0), ("st", 1),
    ("cT", 0), ("h", 3), ("stm", 1), ("pv1", 4), ("pv1", 5), ("s", 2), ("pv0", 1), ("wb", 6), ("f", 0), ("v",
    2), ("wb", 7), ("wb", 8), ("pv1", 6), ("st", 2), ("cT", 1), ("stm", 2), ("v", 3), ("wb", 9), ("pv1", 7),
    ("wb", 10), ("s", 3), ("pv1", 8), ("wb", 11), ("pv0", 2), ("f", 1), ("st", 3), ("gate", 3), ("pv1", 9),
    ("stm", 3), ("pv1", 10), ("pv1", 11), ("maskT", 0), ("cT", 2), ("pv0", 3), ("f", 2), ("cT", 3), ("maskT",
    1), ("f", 3),
]
ACT_ORDER = [
    ("x1hi", 0), ("xhi", 0), ("xhi", 1), ("xhi", 2), ("xhi", 3), ("hout", 0), ("gatet", 0), ("x1hi", 1),
    ("masks", 0), ("qkhi", 0), ("pqw", 0), ("qkhi", 1), ("hout", 1), ("wout", 0), ("gatet", 1), ("wout", 1),
    ("wout", 2), ("qkhi", 2), ("x1hi", 2), ("pqw", 1), ("qkhi", 3), ("hout", 2), ("wout", 3), ("qkhi", 4),
    ("qkhi", 5), ("vout", 0), ("wout", 4), ("exp", 0), ("elu", 0), ("wout", 5), ("x1hi", 3), ("gatet", 2),
    ("vout", 1), ("chi", 0), ("pqw", 2), ("exp", 1), ("hout", 3), ("wout", 6), ("vout", 2), ("wout", 7),
    ("wout", 8), ("pqw", 3), ("chi", 1), ("elu", 1), ("vout", 3), ("exp", 2), ("wout", 9), ("wout", 10), ("elu",
    2), ("wout", 11), ("exp", 3), ("gatet", 3), ("chi", 2), ("elu", 3), ("chi", 3),
]
DVE_ORDER = [
    ("x1lo", 0), ("xlo", 0), ("xlo", 1), ("xlo", 2), ("xlo", 3), ("sd", 0), ("x1lo", 1), ("qklo", 0), ("sda",
    0), ("wlog", 0), ("qklo", 1), ("e", 0), ("e", 1), ("e", 2), ("sd", 1), ("rden1", 0), ("sda", 1), ("wlog",
    1), ("x1lo", 2), ("qklo", 2), ("qklo", 3), ("f_raw", 0), ("e", 3), ("qklo", 4), ("qklo", 5), ("sd", 2),
    ("sda", 2), ("max", 0), ("wlog", 2), ("e", 4), ("max", 1), ("mixa", 0), ("mixb", 0), ("rden0", 0), ("x1lo",
    3), ("ctx0", 0), ("sum1", 0), ("e", 5), ("clo", 0), ("sd", 3), ("rden1", 1), ("max", 2), ("sda", 3),
    ("f_raw", 1), ("rden0", 1), ("e", 6), ("wlog", 3), ("sum0", 0), ("ctx0", 1), ("stats1", 0), ("stats0", 0),
    ("e", 7), ("mv1", 0), ("e", 8), ("clo", 1), ("mixa", 1), ("max", 3), ("rden1", 2), ("e", 9), ("f_raw", 2),
    ("mixb", 1), ("out", 0), ("mv0", 0), ("e", 10), ("sum1", 1), ("sum0", 1), ("stats1", 1), ("rden0", 2),
    ("mv1", 1), ("mixa", 2), ("mixb", 2), ("sum1", 2), ("ctx0", 2), ("stats0", 1), ("e", 11), ("stats1", 2),
    ("x1", 0), ("mv1", 2), ("out", 1), ("mv0", 1), ("rden1", 3), ("f_raw", 3), ("clo", 2), ("x1", 1), ("rden0",
    3), ("clip", 0), ("ctx0", 3), ("sum0", 2), ("stats0", 2), ("clo", 3), ("mixa", 3), ("mv0", 2), ("mixb", 3),
    ("sum1", 3), ("sum0", 3), ("stats0", 3), ("stats1", 3), ("mv0", 3), ("clip", 1), ("mv1", 3), ("x1", 2),
    ("out", 2), ("x1", 3), ("out", 3),
]
POOL_ORDER = [
    ("prod", 0), ("prod", 1), ("prod", 2), ("diag", 0), ("fb", 0), ("ex", 0), ("diag", 1), ("prod", 3),
    ("x_res", 0), ("diag", 2), ("fb", 1), ("ex", 1), ("rstd1", 0), ("fb", 2), ("ex", 2), ("rstd0", 0), ("diag",
    3), ("rstd1", 1), ("rstd0", 1), ("fb", 3), ("rstd1", 2), ("ex", 3), ("rstd0", 2), ("rstd0", 3), ("rstd1", 3),
]
LAYER0 = {"xT", "qk", "s", "st", "stm", "v", "pv0", "cT", "f", "maskT", "masks", "xhi", "qkhi", "vout", "exp", "chi",
          "xlo", "qklo", "max", "rden0", "ctx0", "clo", "sum0", "stats0", "mv0", "x1", "clip", "x_res", "diag", "rstd0"}


def upto(group, per, k):
    return group * per + k


def bass_graph_transformer_gat(nc, x, adj, Wq, bq, Wk, bk, Wv, bv, Wf, bf, W1, b1, w_src, w_dst, H_w, H_b, out):
    graphs, nodes, D = x.shape
    NG = graphs // GROUP
    KT = D // P
    H0, HD0 = 6, 64
    H1, _, HD1 = W1.shape
    PAIRS = H0 // 2
    GN = GROUP * P
    SCALE = float(HD0) ** -0.5
    HI, LO = 0, 1
    THIRDS = 3
    THREE = ((HI, HI), (HI, LO), (LO, HI))
    assert nodes == P and KT * P == D and H0 * HD0 == D and H1 * HD1 == D

    with ExitStack() as ctx:
        def sb(name, shape, dt=F32):
            return ctx.enter_context(nc.sbuf_tensor(name, shape, dt))

        def psum(name, shape, dt=F32):
            return ctx.enter_context(nc.psum_tensor(name, shape, dt))

        def sem(name):
            return ctx.enter_context(nc.semaphore(name))

        t_bank = [psum(f"t_bank{i}", [P, 512]) for i in range(2)]
        p_bank = [psum(f"p_bank{i}", [P, 512]) for i in range(2)]
        scores = psum("scores", [P, 2, 512])
        context0 = psum("context0", [P, 512])
        context1 = psum("context1", [P, 512])

        names = ("q", "k", "v", "f", "h", "g")
        w = {n: sb(f"w_{n}", [P, 2, KT, D], F32R) for n in names}
        ident = sb("ident", [P, P])
        ones_r = sb("ones_r", [P, P], F32R)
        ident_b = sb("ident_b", [P, P], BF16)
        ones_b = sb("ones_b", [P, P], BF16)
        bias_q = sb("bias_q", [P, 2, PAIRS])
        bias_v = sb("bias_v", [P, KT])
        bias_f = sb("bias_f", [P, D])
        out_bias = sb("out_bias", [P, D])
        bias_1 = sb("bias_1", [P, HD1])
        w_sd = sb("w_sd", [P, 2, D])
        sd_shift = sb("sd_shift", [P, 2, H1])
        gate_bias = sb("gate_bias", [P, D])
        gate_bias_parts = sb("gate_bias_parts", [P, D], BF16)
        eps0 = sb("eps0", [P, 1])
        eps1 = sb("eps1", [P, 1])
        minus_half = sb("minus_half", [P, 1])
        minus_one = sb("minus_one", [P, 1])

        x_in = sb("x_in", [P, GROUP, D])
        x_res = sb("x_res", [P, GROUP, D])
        adj_in = sb("adj_in", [P, GROUP, P], U8)
        adj_b = sb("adj_b", [P, GROUP, P], BF16)
        neg = sb("neg", [P, GROUP, P], BF16)
        xT = sb("xT", [P, 2, KT, GN], F32R)
        qT = sb("qT", [P, 2, PAIRS, GN], F32R)
        kT = sb("kT", [P, 2, PAIRS, GN], F32R)
        v = sb("v", [P, GROUP, H0, HD0 + 1])
        neg_max = sb("neg_max", [P, H0])
        diag = sb("diag", [P, H0, P], F32R)
        probs0 = sb("probs0", [P, 2, 2, PAIRS * P])
        rden0 = sb("rden0", [P, H0])
        ctx0 = sb("ctx0", [P, D])
        cT = sb("cT", [P, 2, KT, P], F32R)
        sum0 = sb("sum0", [P, 2, D])
        stats0 = sb("stats0", [P, GROUP, 6])
        mv0 = sb("mv0", [P, GROUP, 2])
        ve0 = sb("ve0", [P, GROUP])
        rstd0 = sb("rstd0", [P, GROUP])
        x1 = sb("x1", [P, GROUP, D])
        clip = sb("clip", [P, GROUP, P])
        x1T = sb("x1T", [P, 2, KT, P], F32R)
        th = sb("th", [P, D])
        h = sb("h", [P, 2, H1, HD1 + 1])
        gate_t = sb("gate_t", [P, 2, D])
        prod = sb("prod", [P, 2, D])
        sd = sb("sd", [P, 2, H1])
        sda = sb("sda", [P, 2, H1])
        wlog = sb("wlog", [P, H1])
        pqw = sb("pqw", [P, 2, 3, H1])
        w_all = sb("w_all", [P, H1, P])
        weights = sb("weights", [P, H1, P])
        rden1 = sb("rden1", [P, H1])
        f_raw = sb("f_raw", [P, D])
        f_b = sb("f_b", [P, 2, D])
        f_neg = sb("f_neg", [P, D])
        f_exp = sb("f_exp", [P, D])
        exp_less_x = sb("exp_less_x", [P, D])
        mix = sb("mix", [P, D])
        sum1 = sb("sum1", [P, 2, D])
        stats1 = sb("stats1", [P, GROUP, 6])
        mv1 = sb("mv1", [P, GROUP, 2])
        ve1 = sb("ve1", [P, GROUP])
        rstd1 = sb("rstd1", [P, GROUP])
        y_out = sb("y_out", [P, 2, D])
        stage = {"q": w_all, "k": weights, "v": x_res, "f": probs0, "h": x1, "g": y_out}
        stage_ap = {
            "q": w_all[:].rearrange("p h i -> p (h i)")[:, 0:KT * D],
            "k": weights[:].rearrange("p h i -> p (h i)")[:, 0:KT * D],
            "v": x_res[:].rearrange("p g d -> p (g d)")[:, 0:KT * D],
            "f": probs0[:].rearrange("p a b c -> p (a b c)")[:, 0:KT * D],
            "h": x1[:].rearrange("p g d -> p (g d)")[:, 0:KT * D],
        }
        stage_g = sb("stage_g", [P, KT, D])
        stage_ap["g"] = stage_g[:].rearrange("p k n -> p (k n)")
        stage_ap = {n: a.rearrange("p (k n) -> p k n", k=KT) for n, a in stage_ap.items()}
        dmas = {n: sem(f"w_{n}_loaded") for n in names}

        s_const = sem("const_made")
        s_bias = sem("bias_loaded")
        s_whi = sem("w_hi_made")
        s_wlo = sem("w_lo_made")
        s_gT = sem("g_transposed")
        s_gTlo = sem("g_lo_made")
        s_ob = sem("out_bias_summed")
        s_prep = sem("prep_done")
        s_link = sem("prep_link")
        s_pool = sem("pool_prep")
        s_free = sem("inputs_free")
        s_x = sem("x_loaded")
        s_adj = sem("adj_loaded")
        s_store = [sem(f"stored{i}") for i in range(2)]
        pe = {n: sem(f"pe_{n}") for n in ("xT", "qk", "s", "v", "st", "pv0", "cT", "f", "maskT",
                                           "x1T", "h", "gate", "wb", "pv1")}
        s_neg = sem("neg_made")
        s_adjb = sem("adj_b_made")
        s_xhi = sem("x_hi_made")
        s_qkhi = sem("qk_hi_made")
        s_v = sem("v_copied")
        s_exp = sem("probs0_made")
        s_chi = sem("c_hi_made")
        s_x1hi = sem("x1_hi_made")
        s_th = sem("th_made")
        s_h = sem("h_copied")
        s_gate = sem("gate_made")
        s_pqw = sem("pqw_made")
        s_wall = sem("w_all_copied")
        s_fneg = sem("f_neg_made")
        s_elu = sem("f_exp_made")
        s_xlo = sem("x_lo_made")
        s_qklo = sem("qk_lo_made")
        s_max = sem("max_found")
        s_rden0 = sem("rden0_made")
        s_ctx0 = sem("ctx0_made")
        s_clo = sem("c_lo_made")
        s_sum0 = sem("sum0_made")
        s_st0 = sem("stats0_made")
        s_seen = sem("stats_seen")
        s_mv0 = sem("mv0_made")
        s_x1 = sem("x1_made")
        s_mx = sem("clip_made")
        s_x1lo = sem("x1_lo_made")
        s_sd = sem("sd_made")
        s_sda = sem("sd_shifted")
        s_wlog = sem("w_exponent_made")
        s_e = sem("weights_clipped")
        s_rden1 = sem("rden1_made")
        s_fraw = sem("f_made")
        s_mixa = sem("mixa_made")
        s_mixb = sem("mixb_made")
        s_sum1 = sem("sum1_made")
        s_st1 = sem("stats1_made")
        s_mv1 = sem("mv1_made")
        s_y = sem("y_made")
        s_xb = sem("x_res_made")
        s_ve0 = sem("var_eps0_made")
        s_rstd0 = sem("rstd0_made")
        s_prod = sem("prod_made")
        s_fb = sem("f_b_made")
        s_ex = sem("exp_less_x_made")
        s_diag = sem("diag_made")
        s_ve1 = sem("var_eps1_made")
        s_rstd1 = sem("rstd1_made")

        x_dram = x.rearrange("g p d -> p g d")
        out_dram = out.rearrange("g p d -> p g d")
        adj_dram = adj.rearrange("g p m -> p g m")

        def wait(eng, s, n):
            if not isinstance(n, int) or n > 0:
                eng.wait_ge(s, n)

        def phases(eng, step, order):
            for name, k in order:
                if name in LAYER0:
                    step(name, k, 0, None)
            for name, k in order:
                step(name, k, 1, 0)
            with eng.Fori(1, NG - 1) as u:
                for name, k in order:
                    step(name, k, u + 1, u)
            for name, k in order:
                if name not in LAYER0:
                    step(name, k, None, NG - 1)

        def heads0(ap):
            return ap.rearrange("p (b j) -> p b j", b=2)

        def over_heads(ap, n):
            return ap.unsqueeze(1).broadcast_to([P, n, ap.shape[-1]])

        def per_head(ap, n):
            return ap.unsqueeze(2).broadcast_to([P, ap.shape[-1], n])

        block = ctx.enter_context(nc.Block())

        @block.sync
        def _(sp):
            sp.dma_start(x_in[:], x_dram[:, 0:GROUP, :]).then_inc(s_x, 16)
            sp.dma_start(adj_in[:], adj_dram[:, 0:GROUP, :]).then_inc(s_adj, 16)
            for n, src in (("q", Wq), ("k", Wk), ("v", Wv), ("f", Wf), ("g", H_w)):
                sp.dma_start(stage_ap[n], src.rearrange("(k p) n -> p k n", p=P)).then_inc(dmas[n], 16)
            for kt in range(KT):
                sp.dma_start(stage_ap["h"][:, kt, :].rearrange("p (a e) -> p a e", a=H1),
                             W1[:, kt * P:(kt + 1) * P, :].rearrange("a p e -> p a e")).then_inc(dmas["h"], 16)

            def at(n):
                return n if isinstance(n, int) else sp.snap(n)

            def load(t):
                first = at(t * GROUP)
                sp.wait_ge(pe["xT"], upto(t, GROUP, 0))
                sp.wait_ge(s_xb, upto(t, 1, 0))
                sp.wait_ge(s_adjb, upto(t, 1, 0))
                sp.sem_inc(s_free, 1)
                sp.dma_start(x_in[:], x_dram[:, bass.ds(first, GROUP), :]).then_inc(s_x, 16)
                sp.dma_start(adj_in[:], adj_dram[:, bass.ds(first, GROUP), :]).then_inc(s_adj, 16)

            def store(t):
                for g in range(GROUP):
                    graph = at(t * GROUP + g)
                    sp.wait_ge(s_y, upto(t, GROUP, g + 1))
                    sp.dma_start(out_dram[:, bass.ds(graph, 1), :],
                                 y_out[:, g % 2, :].unsqueeze(1)).then_inc(s_store[g % 2], 16)

            load(1)
            load(2)
            store(0)
            with sp.Fori(1, NG - 2) as u:
                load(u + 2)
                store(u)
            store(NG - 2)
            store(NG - 1)
            for g in range(2):
                sp.wait_ge(s_store[g], graphs // 2 * 16)

        @block.tensor
        def _(te):
            te.wait_ge(s_const, 3)
            te.wait_ge(dmas["g"], 16)
            for kt in range(KT):
                if kt >= 2:
                    te.wait_ge(s_gTlo, kt - 1)
                for ot in range(KT):
                    last = te.transpose(t_bank[kt % 2][:, ot * P:(ot + 1) * P],
                                        stage_ap["g"][:, ot, kt * P:(kt + 1) * P], ident[:])
                last.then_inc(s_gT, 1)
            te.wait_ge(s_bias, 7 * 16)
            te.wait_ge(dmas["f"], 16)
            for kt in range(KT):
                last = te.matmul(p_bank[0][:, 0:D], bias_v[:, kt:kt + 1].broadcast_to([P, P]),
                                 stage_ap["f"][:, kt, :], start=(kt == 0), stop=(kt == KT - 1))
            last.then_inc(s_ob, 1)
            te.wait_ge(s_prep, 1)

            t_freed = {"xT": (s_xlo, GROUP), "x1T": (s_x1lo, GROUP), "cT": (s_clo, GROUP),
                       "wb": (s_wall, THIRDS * GROUP), "maskT": (s_mx, 2)}
            p_freed = {"qk": (s_qklo, 2 * PAIRS), "v": (s_v, GROUP), "f": (s_sum0, GROUP),
                       "h": (s_h, GROUP), "gate": (s_gate, GROUP)}

            def uses(freed, phase):
                return bank_uses(PE_ORDER, freed, phase)

            def bank(banks, freed, name, k, g0, g1):
                order = uses(freed, "first" if g1 is None else "last" if g0 is None else "loop")
                at = order.index((name, k))
                if at >= 2:
                    before, kb = order[at - 2]
                    s, per = freed[before]
                    te.wait_ge(s, upto(g0 if before in LAYER0 else g1, per, kb + 1))
                elif g1 is not None:
                    before, kb = uses(freed, "loop")[at - 2]
                    assert before in LAYER0
                    s, per = freed[before]
                    te.wait_ge(s, upto(g1, per, kb + 1))
                return banks[at % 2]

            def project(dst, left, right, opened=False):
                n = 0
                for kt in range(KT):
                    for a, b in THREE:
                        last = te.matmul(dst, left(a, kt), right(b, kt), start=(n == 0 and not opened),
                                         stop=(n == 3 * KT - 1))
                        n += 1
                return last

            def head(ap, part, j, b, g):
                return ap[b * HD0:(b + 1) * HD0, part, j, g * P:(g + 1) * P]

            def step(name, k, g0, g1):
                if name == "xT":
                    if k == 0:
                        te.wait_ge(s_x, upto(g0, 16, 16))
                    dst = bank(t_bank, t_freed, name, k, g0, g1)
                    for kt in range(KT):
                        last = te.transpose(dst[:, kt * P:(kt + 1) * P], x_in[:, k, kt * P:(kt + 1) * P], ident[:])
                    last.then_inc(pe["xT"], 1)
                elif name == "qk":
                    if k == 0:
                        te.wait_ge(s_xlo, upto(g0, GROUP, GROUP))
                    dst = bank(p_bank, p_freed, name, k, g0, g1)
                    j, m = k // 2, w["qk"[k % 2]]
                    project(dst[:, :], lambda a, kt: m[:, a, kt, j * P:(j + 1) * P],
                            lambda b, kt: xT[:, b, kt, :]).then_inc(pe["qk"], 1)
                elif name == "v":
                    dst = bank(p_bank, p_freed, name, k, g0, g1)
                    project(dst[:, 0:D], lambda a, kt: xT[:, a, kt, k * P:(k + 1) * P],
                            lambda b, kt: w["v"][:, b, kt, :]).then_inc(pe["v"], 1)
                elif name == "s":
                    if k == 0:
                        te.wait_ge(s_qklo, upto(g0, 2 * PAIRS, 2 * PAIRS))
                        te.wait_ge(s_neg, upto(g0, 1, 1))
                    wait(te, s_exp, upto(g0, GROUP, k))
                    for b in range(2):
                        te.matmul(scores[:, b, 0:PAIRS * P], ident_b[:], over_heads(neg[:, k, :], PAIRS),
                                  start=True, stop=False)
                    for j in range(PAIRS):
                        for b in range(2):
                            last = te.matmul(scores[:, b, j * P:(j + 1) * P], head(qT, HI, j, b, k),
                                             head(kT, HI, j, b, k), start=False, stop=(j == PAIRS - 1))
                    last.then_inc(pe["s"], 1)
                elif name == "st":
                    te.wait_ge(s_max, upto(g0, GROUP, k + 1))
                    for b in range(2):
                        te.matmul(scores[:, b, 0:PAIRS * P], neg[:, k, :], over_heads(ident_b[:], PAIRS),
                                  start=True, stop=False)
                    for a, c in THREE:
                        for j in range(PAIRS):
                            for b in range(2):
                                te.matmul(scores[:, b, j * P:(j + 1) * P], head(kT, a, j, b, k),
                                          head(qT, c, j, b, k), start=False, stop=False)
                elif name == "stm":
                    te.wait_ge(s_diag, upto(g0, GROUP, k + 1))
                    for b in range(2):
                        last = te.matmul(scores[:, b, 0:PAIRS * P], ones_r[:],
                                         diag[:, b * PAIRS:(b + 1) * PAIRS, :].rearrange("p h n -> p (h n)"),
                                         start=False, stop=True)
                    last.then_inc(pe["st"], 1)
                elif name == "pv0":
                    te.wait_ge(s_exp, upto(g0, GROUP, k + 1))
                    te.wait_ge(s_v, upto(g0, GROUP, k + 1))
                    wait(te, s_ctx0, upto(g0, GROUP, k))
                    for j in range(PAIRS):
                        for b in range(2):
                            n = 2 * j + b
                            last = te.matmul(context0[:, n * (HD0 + 1):(n + 1) * (HD0 + 1)],
                                             probs0[:, k % 2, b, j * P:(j + 1) * P], v[:, k, n, :],
                                             start=True, stop=True)
                    last.then_inc(pe["pv0"], 1)
                elif name == "cT":
                    te.wait_ge(s_ctx0, upto(g0, GROUP, k + 1))
                    dst = bank(t_bank, t_freed, name, k, g0, g1)
                    for kt in range(KT):
                        last = te.transpose(dst[:, kt * P:(kt + 1) * P], ctx0[:, kt * P:(kt + 1) * P], ident[:])
                    last.then_inc(pe["cT"], 1)
                elif name == "f":
                    te.wait_ge(s_clo, upto(g0, GROUP, k + 1))
                    dst = bank(p_bank, p_freed, name, k, g0, g1)
                    project(dst[:, 0:D], lambda a, kt: cT[:, a, kt, :],
                            lambda b, kt: w["f"][:, b, kt, :]).then_inc(pe["f"], 1)
                elif name == "maskT":
                    dst = bank(t_bank, t_freed, name, k, g0, g1)
                    if k == 0:
                        te.wait_ge(s_adjb, upto(g0, 1, 1))
                    for i in range(2):
                        last = te.transpose(dst[:, 0:P].bitcast(BF16)[:, i * P:(i + 1) * P],
                                            adj_b[:, 2 * k + i, :], ident_b[:])
                    last.then_inc(pe["maskT"], 1)
                elif name == "x1T":
                    te.wait_ge(s_x1, upto(g1, GROUP, k + 1))
                    dst = bank(t_bank, t_freed, name, k, g0, g1)
                    for kt in range(KT):
                        last = te.transpose(dst[:, kt * P:(kt + 1) * P], x1[:, k, kt * P:(kt + 1) * P], ident[:])
                    last.then_inc(pe["x1T"], 1)
                elif name == "h":
                    te.wait_ge(s_x1lo, upto(g1, GROUP, k + 1))
                    dst = bank(p_bank, p_freed, name, k, g0, g1)
                    project(dst[:, 0:D], lambda a, kt: x1T[:, a, kt, :],
                            lambda b, kt: w["h"][:, b, kt, :]).then_inc(pe["h"], 1)
                elif name == "gate":
                    dst = bank(p_bank, p_freed, name, k, g0, g1)
                    te.matmul(dst[:, 0:D], ones_b[:], gate_bias_parts[:], start=True, stop=False)
                    project(dst[:, 0:D], lambda a, kt: x1T[:, a, kt, :],
                            lambda b, kt: w["g"][:, b, kt, :], opened=True).then_inc(pe["gate"], 1)
                elif name == "wb":
                    g, r = divmod(k, THIRDS)
                    te.wait_ge(s_pqw, upto(g1, 3 * GROUP, 3 * g + 3))
                    dst = bank(t_bank, t_freed, name, k, g0, g1)
                    for i in range(H1 // THIRDS):
                        n = H1 // THIRDS * r + i
                        last = te.transpose(dst[:, i * P:(i + 1) * P],
                                            pqw[:, g % 2, 2, n:n + 1].broadcast_to([P, P]), ident[:])
                    last.then_inc(pe["wb"], 1)
                elif name == "pv1":
                    g, r = divmod(k, THIRDS)
                    te.wait_ge(s_e, upto(g1, THIRDS * GROUP, k + 1))
                    te.wait_ge(s_h, upto(g1, GROUP, g + 1))
                    wait(te, s_fraw, upto(g1, GROUP, g))
                    for n in range(H1 // THIRDS * r, H1 // THIRDS * (r + 1)):
                        last = te.matmul(context1[:, n * (HD1 + 1):(n + 1) * (HD1 + 1)], weights[:, n, :],
                                         h[:, g % 2, n, :], start=True, stop=True)
                    last.then_inc(pe["pv1"], 1)

            phases(te, step, PE_ORDER)

        @block.scalar
        def _(act):
            for n, src in ((0, bq), (1, bk)):
                act.dma_start(bias_q[:, n, :], src.rearrange("(m p) -> p m", p=P), allow_slow_non_contiguous=True).then_inc(s_bias, 16)
            act.dma_start(bias_v[:], bv.rearrange("(m p) -> p m", p=P), allow_slow_non_contiguous=True).then_inc(s_bias, 16)
            act.dma_start(bias_f[:], bf.partition_broadcast(P)).then_inc(s_bias, 16)
            act.dma_start(bias_1[:], b1.partition_broadcast(P)).then_inc(s_bias, 16)
            act.dma_start(w_sd[:, 0, :], w_src.rearrange("a e o -> (a e o)").partition_broadcast(P)).then_inc(s_bias, 16)
            act.dma_start(gate_bias[:], H_b.partition_broadcast(P)).then_inc(s_bias, 16)
            act.dma_start(w_sd[:, 1, :], w_dst.rearrange("a e o -> (a e o)").partition_broadcast(P)).then_inc(s_bias, 16)
            act.wait_ge(s_const, 4)
            act.activation(ident_b[:], ident[:], ACT.Copy).then_inc(s_link, 1)
            act.activation(ones_r[:], ones_b[:], ACT.Copy).then_inc(s_link, 1)
            act.activation(ve0[:, 0:1], eps0[:], ACT.Exp).then_inc(s_link, 1)
            for n in ("q", "k", "v", "h", "f"):
                act.wait_ge(dmas[n], 16 * KT if n == "h" else 16)
                act.activation(w[n][:, HI], stage_ap[n], ACT.Copy).then_inc(s_whi, 1)
            for kt in range(KT):
                act.wait_ge(s_gT, kt + 1)
                act.activation(w["g"][:, HI, kt, :], t_bank[kt % 2][:, 0:D], ACT.Copy).then_inc(s_whi, 1)
            act.wait_ge(s_prep, 1)

            def step(name, k, g0, g1):
                if name == "masks":
                    act.wait_ge(s_adj, upto(g0, 16, 16))
                    wait(act, pe["st"], upto(g0, GROUP, 0))
                    act.activation(neg[:], adj_in[:], ACT.Copy, scale=-MASKED, bias=MASKED).then_inc(s_neg, 1)
                    wait(act, pe["maskT"], upto(g0, 2, 0))
                    act.activation(adj_b[:], adj_in[:], ACT.Copy).then_inc(s_adjb, 1)
                elif name == "xhi":
                    act.wait_ge(pe["xT"], upto(g0, GROUP, k + 1))
                    if k == 0:
                        wait(act, pe["v"], upto(g0, GROUP, 0))
                        wait(act, pe["qk"], upto(g0, 2 * PAIRS, 0))
                    act.activation(xT[:, HI, :, k * P:(k + 1) * P],
                                   t_bank[t_at("xT", k, g1)][:, 0:D].rearrange("p (k n) -> p k n", k=KT),
                                   ACT.Copy).then_inc(s_xhi, 1)
                elif name == "qkhi":
                    act.wait_ge(pe["qk"], upto(g0, 2 * PAIRS, k + 1))
                    if k == 0:
                        wait(act, pe["st"], upto(g0, GROUP, 0))
                    dst = (qT, kT)[k % 2]
                    act.activation(dst[:, HI, k // 2, :], p_bank[p_at("qk", k, g1)][:, :], ACT.Identity,
                                   bias=bias_q[:, k % 2, k // 2:k // 2 + 1]).then_inc(s_qkhi, 1)
                elif name == "vout":
                    act.wait_ge(pe["v"], upto(g0, GROUP, k + 1))
                    wait(act, pe["pv0"], upto(g0, GROUP, k + 1 - GROUP))
                    act.activation(v[:, k, :, 0:HD0],
                                   p_bank[p_at("v", k, g1)][:, 0:D].rearrange("p (h e) -> p h e", h=H0),
                                   ACT.Copy).then_inc(s_v, 1)
                elif name == "exp":
                    act.wait_ge(pe["st"], upto(g0, GROUP, k + 1))
                    wait(act, pe["pv0"], upto(g0, GROUP, k - 1))
                    act.activation(probs0[:, k % 2], scores[:, :, 0:PAIRS * P], ACT.Exp,
                                   scale=SCALE).then_inc(s_exp, 1)
                elif name == "chi":
                    act.wait_ge(pe["cT"], upto(g0, GROUP, k + 1))
                    wait(act, pe["f"], upto(g0, GROUP, k))
                    act.activation(cT[:, HI], t_bank[t_at("cT", k, g1)][:, 0:D].rearrange("p (k n) -> p k n", k=KT),
                                   ACT.Copy).then_inc(s_chi, 1)
                elif name == "x1hi":
                    act.wait_ge(pe["x1T"], upto(g1, GROUP, k + 1))
                    wait(act, pe["gate"], upto(g1, GROUP, k))
                    act.activation(x1T[:, HI], t_bank[t_at("x1T", k, g1, g0)][:, 0:D].rearrange("p (k n) -> p k n", k=KT),
                                   ACT.Copy).then_inc(s_x1hi, 1)
                elif name == "hout":
                    src = p_bank[p_at("h", k, g1, g0)][:, 0:D]
                    act.wait_ge(pe["h"], upto(g1, GROUP, k + 1))
                    wait(act, s_prod, upto(g1, GROUP, k))
                    act.activation(th[:], src, ACT.Tanh).then_inc(s_th, 1)
                    wait(act, pe["pv1"], upto(g1, THIRDS * GROUP, THIRDS * (k - 1)))
                    act.activation(h[:, k % 2, :, 0:HD1], src.rearrange("p (h e) -> p h e", h=H1),
                                   ACT.Copy).then_inc(s_h, 1)
                elif name == "gatet":
                    act.wait_ge(pe["gate"], upto(g1, GROUP, k + 1))
                    wait(act, s_sum1, upto(g1, GROUP, k - 1))
                    act.activation(gate_t[:, k % 2, :], p_bank[p_at("gate", k, g1, g0)][:, 0:D], ACT.Tanh,
                                   scale=0.5).then_inc(s_gate, 1)
                elif name == "pqw":
                    act.wait_ge(s_sda, upto(g1, GROUP, k + 1))
                    wait(act, s_e, upto(g1, THIRDS * GROUP, THIRDS * (k - 1)))
                    act.activation(pqw[:, k % 2, 0, :], sda[:, 1, :], ACT.Exp).then_inc(s_pqw, 1)
                    act.activation(pqw[:, k % 2, 1, :], sda[:, 1, :], ACT.Exp, scale=LEAKY).then_inc(s_pqw, 1)
                    act.wait_ge(s_wlog, upto(g1, GROUP, k + 1))
                    wait(act, pe["wb"], upto(g1, THIRDS * GROUP, THIRDS * (k - 1)))
                    act.activation(pqw[:, k % 2, 2, :], wlog[:], ACT.Exp, scale=LEAKY - 1.0).then_inc(s_pqw, 1)
                elif name == "wout":
                    g, r = divmod(k, THIRDS)
                    wait(act, s_e, upto(g1, THIRDS * GROUP, k + 1 - THIRDS))
                    act.wait_ge(s_pqw, upto(g1, 3 * GROUP, 3 * g + 2))
                    act.wait_ge(pe["wb"], upto(g1, THIRDS * GROUP, k + 1))
                    src = t_bank[t_at("wb", k, g1, g0)]
                    for i in range(H1 // THIRDS):
                        n = H1 // THIRDS * r + i
                        last = act.activation(w_all[:, n, :], src[:, i * P:(i + 1) * P], ACT.Copy,
                                              scale=pqw[:, g % 2, 1, n:n + 1])
                    last.then_inc(s_wall, 1)
                elif name == "elu":
                    wait(act, s_elu, upto(g1, GROUP, k))
                    act.wait_ge(s_fb, upto(g1, GROUP, k + 1))
                    act.activation(f_neg[:], f_b[:, k % 2, :], ACT.Relu, scale=-1.0,
                                   bias=minus_one[:]).then_inc(s_fneg, 1)
                    act.wait_ge(s_fneg, upto(g1, GROUP, k + 1))
                    wait(act, s_ex, upto(g1, GROUP, k))
                    act.activation(f_exp[:], f_neg[:], ACT.Exp, scale=-1.0).then_inc(s_elu, 1)

            phases(act, step, ACT_ORDER)

        @block.vector
        def _(dve):
            linked = [0]

            def link(ins):
                linked[0] += 1
                ins.then_inc(s_pool, 1)
                dve.wait_ge(s_pool, linked[0])

            dve.memset(v[:, :, :, HD0:HD0 + 1], 1.0)
            dve.memset(h[:, :, :, HD1:HD1 + 1], 1.0)
            dve.memset(eps1[:], LN_EPS / 4)
            dve.memset(minus_one[:], -1.0)
            link(dve.memset(gate_bias_parts[:], 0.0))
            dve.wait_ge(s_bias, 8 * 16)
            rest = mix
            link(dve.tensor_copy(gate_bias_parts[0:1, :], gate_bias[0:1, :]))
            part = prod[:].rearrange("p a d -> p (a d)").bitcast(BF16)[:, 0:D]
            link(dve.tensor_copy(part, gate_bias[:]))
            link(dve.tensor_tensor(rest[:], gate_bias[:], part, ALU.subtract))
            link(dve.tensor_copy(gate_bias_parts[32:33, :], rest[32:33, :]))
            link(dve.tensor_copy(part, rest[:]))
            link(dve.tensor_tensor(rest[:], rest[:], part, ALU.subtract))
            link(dve.tensor_copy(gate_bias_parts[64:65, :], rest[64:65, :]))
            link(dve.tensor_reduce(sd_shift[:, 0, :], w_sd[:, 1, :].rearrange("p (h e) -> p h e", h=H1), AX_X,
                                   ALU.add, apply_absolute_value=True))
            link(dve.tensor_scalar(sd_shift[:, 0, :], sd_shift[:, 0, :], -EXP_ROOM, 0.0, ALU.add, ALU.max))
            link(dve.tensor_scalar(sd_shift[:, 1, :], sd_shift[:, 0, :], -1.0, None, ALU.mult))
            link(dve.tensor_scalar(bias_1[:], bias_1[:], -1.0, None, ALU.add))
            for i, n in enumerate(("q", "k", "v", "h", "f")):
                dve.wait_ge(s_whi, i + 1)
                dve.tensor_tensor(w[n][:, LO], stage_ap[n], w[n][:, HI].bitcast(F32), ALU.subtract).then_inc(s_wlo, 1)
            for kt in range(KT):
                dve.wait_ge(s_whi, 6 + kt)
                dve.tensor_tensor(w["g"][:, LO, kt, :], t_bank[kt % 2][:, 0:D], w["g"][:, HI, kt, :].bitcast(F32),
                                  ALU.subtract).then_inc(s_gTlo, 1)
            dve.wait_ge(s_ob, 1)
            link(dve.tensor_tensor(out_bias[:], p_bank[0][:, 0:D], bias_f[:], ALU.add))
            dve.wait_ge(s_wlo, 5)
            dve.wait_ge(s_gTlo, KT)
            dve.wait_ge(s_link, 3)
            dve.memset(ve1[:], 0.0).then_inc(s_prep, 1)

            def low(dst, src, hi):
                return dve.tensor_tensor(dst, src, hi.bitcast(F32), ALU.subtract)

            sums0 = context0[:, 0:H0 * (HD0 + 1)].rearrange("p (h e) -> p h e", h=H0)
            sums1 = context1[:, 0:H1 * (HD1 + 1)].rearrange("p (h e) -> p h e", h=H1)

            def step(name, k, g0, g1):
                if name == "xlo":
                    dve.wait_ge(s_xhi, upto(g0, GROUP, k + 1))
                    cols = slice(k * P, (k + 1) * P)
                    low(xT[:, LO, :, cols], t_bank[t_at("xT", k, g1)][:, 0:D].rearrange("p (k n) -> p k n", k=KT),
                        xT[:, HI, :, cols]).then_inc(s_xlo, 1)
                elif name == "qklo":
                    dve.wait_ge(s_qkhi, upto(g0, 2 * PAIRS, k + 1))
                    dst = (qT, kT)[k % 2]
                    dve.scalar_tensor_tensor(out=dst[:, LO, k // 2, :], in0=p_bank[p_at("qk", k, g1)][:, :],
                                             scalar=bias_q[:, k % 2, k // 2:k // 2 + 1],
                                             in1=dst[:, HI, k // 2, :].bitcast(F32),
                                             op0=ALU.add, op1=ALU.subtract).then_inc(s_qklo, 1)
                elif name == "max":
                    dve.wait_ge(pe["s"], upto(g0, GROUP, k + 1))
                    wait(dve, s_diag, upto(g0, GROUP, k))
                    dve.tensor_reduce(heads0(neg_max[:]),
                                      scores[:, :, 0:PAIRS * P].rearrange("p b (j n) -> p b j n", j=PAIRS),
                                      AX_X, ALU.max, negate=True).then_inc(s_max, 1)
                elif name == "rden0":
                    dve.wait_ge(pe["pv0"], upto(g0, GROUP, k + 1))
                    dve.reciprocal(rden0[:], sums0[:, :, HD0:HD0 + 1].rearrange("p h o -> p (h o)")).then_inc(s_rden0, 1)
                elif name == "ctx0":
                    dve.wait_ge(s_rden0, upto(g0, GROUP, k + 1))
                    wait(dve, pe["cT"], upto(g0, GROUP, k))
                    dve.tensor_tensor(ctx0[:].rearrange("p (h e) -> p h e", h=H0), sums0[:, :, 0:HD0],
                                      per_head(rden0[:], HD0), ALU.mult).then_inc(s_ctx0, 1)
                elif name == "clo":
                    dve.wait_ge(s_chi, upto(g0, GROUP, k + 1))
                    low(cT[:, LO], t_bank[t_at("cT", k, g1)][:, 0:D].rearrange("p (k n) -> p k n", k=KT),
                        cT[:, HI]).then_inc(s_clo, 1)
                elif name == "sum0":
                    dve.wait_ge(pe["f"], upto(g0, GROUP, k + 1))
                    dve.wait_ge(s_xb, upto(g0, 1, 1))
                    wait(dve, s_x1, upto(g0, GROUP, k - 1))
                    dve.tensor_tensor(sum0[:, k % 2, :], p_bank[p_at("f", k, g1)][:, 0:D], x_res[:, k, :],
                                      ALU.add).then_inc(s_sum0, 1)
                elif name == "stats0":
                    dve.wait_ge(s_sum0, upto(g0, GROUP, k + 1))
                    dve.bn_stats(stats0[:, k, :], sum0[:, k % 2, :]).then_inc(s_st0, 1)
                elif name == "mv0":
                    dve.wait_ge(s_st0, upto(g0, GROUP, k + 1))
                    dve.sem_inc(s_seen, 1)
                    dve.bn_aggr(mv0[:, k, :], stats0[:, k, :]).then_inc(s_mv0, 1)
                elif name == "x1":
                    dve.wait_ge(s_rstd0, upto(g0, GROUP, k + 1))
                    if g1 is not None:
                        dve.wait_ge(s_sum1, upto(g1, GROUP, k + 1))
                    dve.tensor_scalar(x1[:, k, :], sum0[:, k % 2, :], mv0[:, k, 0:1], rstd0[:, k:k + 1],
                                      ALU.subtract, ALU.mult).then_inc(s_x1, 1)
                elif name == "clip":
                    dve.wait_ge(pe["maskT"], upto(g0, 2, k + 1))
                    if g1 is not None:
                        dve.wait_ge(s_e, upto(g1, THIRDS * GROUP, THIRDS * GROUP))
                    src = t_bank[t_at("maskT", k, g1)][:, 0:P].bitcast(BF16).rearrange("p (i n) -> p i n", i=2)
                    dve.tensor_scalar(clip[:, 2 * k:2 * k + 2, :], src, KEEP, FLOOR, ALU.mult, ALU.add).then_inc(s_mx, 1)
                elif name == "x1lo":
                    dve.wait_ge(s_x1hi, upto(g1, GROUP, k + 1))
                    low(x1T[:, LO], t_bank[t_at("x1T", k, g1, g0)][:, 0:D].rearrange("p (k n) -> p k n", k=KT),
                        x1T[:, HI]).then_inc(s_x1lo, 1)
                elif name == "sd":
                    dve.wait_ge(s_prod, upto(g1, GROUP, k + 1))
                    wait(dve, s_sda, upto(g1, GROUP, k))
                    dve.tensor_reduce(sd[:].rearrange("p a h -> p (a h)"),
                                      prod[:].rearrange("p a (h e) -> p (a h) e", h=H1), AX_X,
                                      ALU.add).then_inc(s_sd, 1)
                elif name == "sda":
                    dve.wait_ge(s_sd, upto(g1, GROUP, k + 1))
                    wait(dve, s_pqw, upto(g1, 3 * GROUP, 3 * k))
                    dve.tensor_tensor(sda[:], sd[:], sd_shift[:], ALU.add).then_inc(s_sda, 1)
                elif name == "wlog":
                    dve.wait_ge(s_sda, upto(g1, GROUP, k + 1))
                    dve.tensor_scalar(wlog[:], sda[:, 0, :], -EXP_ROOM, None, ALU.max).then_inc(s_wlog, 1)
                elif name == "e":
                    g, r = divmod(k, THIRDS)
                    dve.wait_ge(s_wall, upto(g1, THIRDS * GROUP, k + 1))
                    wait(dve, pe["pv1"], upto(g1, THIRDS * GROUP, k + 1 - THIRDS))
                    for n in range(H1 // THIRDS * r, H1 // THIRDS * (r + 1)):
                        last = dve.scalar_tensor_tensor(out=weights[:, n, :], in0=w_all[:, n, :],
                                                        scalar=pqw[:, g % 2, 0, n:n + 1], in1=clip[:, g, :],
                                                        op0=ALU.max, op1=ALU.min)
                    last.then_inc(s_e, 1)
                elif name == "rden1":
                    dve.wait_ge(pe["pv1"], upto(g1, THIRDS * GROUP, THIRDS * (k + 1)))
                    dve.reciprocal(rden1[:], sums1[:, :, HD1:HD1 + 1].rearrange("p h o -> p (h o)")).then_inc(s_rden1, 1)
                elif name == "f_raw":
                    dve.wait_ge(s_rden1, upto(g1, GROUP, k + 1))
                    wait(dve, s_fb, upto(g1, GROUP, k))
                    dve.tensor_tensor(f_raw[:].rearrange("p (h e) -> p h e", h=H1), sums1[:, :, 0:HD1],
                                      per_head(rden1[:], HD1), ALU.mult).then_inc(s_fraw, 1)
                elif name == "mixa":
                    dve.wait_ge(s_ex, upto(g1, GROUP, k + 1))
                    wait(dve, s_sum1, upto(g1, GROUP, k))
                    dve.scalar_tensor_tensor(out=mix[:], in0=f_b[:, k % 2, :], scalar=-1.0, in1=exp_less_x[:],
                                             op0=ALU.max, op1=ALU.add).then_inc(s_mixa, 1)
                elif name == "mixb":
                    dve.wait_ge(s_mixa, upto(g1, GROUP, k + 1))
                    dve.wait_ge(s_gate, upto(g1, GROUP, k + 1))
                    dve.scalar_tensor_tensor(out=mix[:], in0=gate_t[:, k % 2, :], scalar=1.0, in1=mix[:],
                                             op0=ALU.add, op1=ALU.mult).then_inc(s_mixb, 1)
                elif name == "sum1":
                    dve.wait_ge(s_mixb, upto(g1, GROUP, k + 1))
                    wait(dve, s_y, upto(g1, GROUP, k - 1))
                    dve.scalar_tensor_tensor(out=sum1[:, k % 2, :], in0=mix[:], scalar=0.25, in1=x1[:, k, :],
                                             op0=ALU.mult, op1=ALU.add).then_inc(s_sum1, 1)
                elif name == "stats1":
                    dve.wait_ge(s_sum1, upto(g1, GROUP, k + 1))
                    dve.bn_stats(stats1[:, k, :], sum1[:, k % 2, :]).then_inc(s_st1, 1)
                elif name == "mv1":
                    dve.wait_ge(s_st1, upto(g1, GROUP, k + 1))
                    dve.sem_inc(s_seen, 1)
                    dve.bn_aggr(mv1[:, k, :], stats1[:, k, :]).then_inc(s_mv1, 1)
                elif name == "out":
                    dve.wait_ge(s_rstd1, upto(g1, GROUP, k + 1))
                    wait(dve, s_store[k % 2], upto(g1, GROUP // 2 * 16, k // 2 * 16))
                    dve.tensor_scalar(y_out[:, k % 2, :], sum1[:, k % 2, :], mv1[:, k, 0:1], rstd1[:, k:k + 1],
                                      ALU.subtract, ALU.mult).then_inc(s_y, 1)

            phases(dve, step, DVE_ORDER)

        @block.gpsimd
        def _(pool):
            pool.memset(ident[:], 0.0).then_inc(s_const, 1)
            pool.memset(ones_b[:], 1.0).then_inc(s_const, 1)
            pool.memset(eps0[:], LN_EPS)
            pool.wait_ge(s_const, 2)
            pool.affine_select(out=ident[:], in_=ident[:], compare_op=ALU.not_equal, fill=1.0, base=0,
                               pattern=[[-1, P]], channel_multiplier=1).then_inc(s_const, 1)
            pool.memset(minus_half[:], -0.5).then_inc(s_const, 1)
            pool.wait_ge(s_prep, 1)

            def rsqrt(mv, ve, rstd, eps, made_mv, made_ve, made_rstd, n):
                pool.wait_ge(made_mv, n)
                pool.tensor_tensor(ve, mv, eps[:], ALU.add).then_inc(made_ve, 1)
                pool.wait_ge(made_ve, n)
                pool.tensor_tensor(rstd, ve, minus_half[:], ALU.pow).then_inc(made_rstd, 1)

            def step(name, k, g0, g1):
                if name == "x_res":
                    pool.wait_ge(s_x, upto(g0, 16, 16))
                    wait(pool, s_sum0, upto(g0, GROUP, 0))
                    pool.tensor_tensor(x_res[:], x_in[:], over_heads(out_bias[:], GROUP), ALU.add).then_inc(s_xb, 1)
                elif name == "rstd0":
                    rsqrt(mv0[:, k, 1:2], ve0[:, k:k + 1], rstd0[:, k:k + 1], eps0, s_mv0, s_ve0, s_rstd0,
                          upto(g0, GROUP, k + 1))
                elif name == "prod":
                    pool.wait_ge(s_th, upto(g1, GROUP, k + 1))
                    wait(pool, s_sd, upto(g1, GROUP, k))
                    pool.tensor_tensor(prod[:], over_heads(th[:], 2), w_sd[:], ALU.mult).then_inc(s_prod, 1)
                elif name == "fb":
                    pool.wait_ge(s_fraw, upto(g1, GROUP, k + 1))
                    wait(pool, s_mixb, upto(g1, GROUP, k - 1))
                    pool.tensor_tensor(f_b[:, k % 2, :].rearrange("p (h e) -> p h e", h=H1),
                                       f_raw[:].rearrange("p (h e) -> p h e", h=H1),
                                       over_heads(bias_1[:], H1), ALU.add).then_inc(s_fb, 1)
                elif name == "ex":
                    pool.wait_ge(s_elu, upto(g1, GROUP, k + 1))
                    wait(pool, s_mixb, upto(g1, GROUP, k))
                    pool.tensor_tensor(exp_less_x[:], f_exp[:], x1[:, k, :], ALU.subtract).then_inc(s_ex, 1)
                elif name == "diag":
                    pool.wait_ge(s_max, upto(g0, GROUP, k + 1))
                    wait(pool, pe["st"], upto(g0, GROUP, k))
                    pool.tensor_tensor(diag[:], over_heads(ident[:], H0), per_head(neg_max[:], P),
                                       ALU.mult).then_inc(s_diag, 1)
                elif name == "rstd1":
                    rsqrt(mv1[:, k, 1:2], ve1[:, k:k + 1], rstd1[:, k:k + 1], eps1, s_mv1, s_ve1, s_rstd1,
                          upto(g1, GROUP, k + 1))

            phases(pool, step, POOL_ORDER)


T_STAGES = {"xT", "x1T", "cT", "wb", "maskT"}
P_STAGES = {"qk", "v", "f", "h", "gate"}


def bank_uses(order, stages, phase):
    return [(n, k) for n, k in order if n in stages and phase != ("last" if n in LAYER0 else "first")]


def bank_of(stages, name, k, first, last):
    return bank_uses(PE_ORDER, stages, "first" if first else "last" if last else "loop").index((name, k)) % 2


def t_at(name, k, g1, g0=0):
    return bank_of(T_STAGES, name, k, g1 is None, g0 is None)


def p_at(name, k, g1, g0=0):
    return bank_of(P_STAGES, name, k, g1 is None, g0 is None)


_INS = ['x', 'adj', 'L0_gnn_Wq', 'L0_gnn_bq', 'L0_gnn_Wk', 'L0_gnn_bk', 'L0_gnn_Wv', 'L0_gnn_bv', 'L0_gnn_Wf',
        'L0_gnn_bf', 'L1_gnn_W', 'L1_gnn_b', 'L1_gnn_w_src', 'L1_gnn_w_dst', 'L1_gnn_H_w', 'L1_gnn_H_b']
_OUTS = [((64, 128, 384), 'float32')]


def kernel(**inputs):
    import numpy as _np
    import concourse.bacc as _bacc
    from concourse import mybir as _mybir
    from concourse.bass_utils import run_bass_kernel_spmd as _run

    nc = _bacc.Bacc("TRN2", target_bir_lowering=False, num_devices=1)
    arrays, args = {}, []
    for name in _INS:
        a = _np.ascontiguousarray(inputs[name])
        arrays[f"in_{name}_dram"] = a
        args.append(nc.dram_tensor(f"in_{name}_dram", a.shape, _mybir.dt.from_np(a.dtype), kind="ExternalInput").ap())
    for i, (shape, dtype) in enumerate(_OUTS):
        dt = _mybir.dt.from_np(_np.dtype(dtype))
        args.append(nc.dram_tensor(f"out_{i}_dram", shape, dt, kind="ExternalOutput").ap())
    bass_graph_transformer_gat(nc, *args)
    r = _run(nc, [arrays], core_ids=[0])
    got = tuple(r.results[0][f"out_{i}_dram"] for i in range(len(_OUTS)))
    return got[0]
```

```python
from contextlib import ExitStack

import concourse.bass as bass
from concourse import mybir

F32 = mybir.dt.float32
F32R = mybir.dt.float32r
BF16 = mybir.dt.bfloat16
U8 = mybir.dt.uint8
ALU = mybir.AluOpType
ACT = mybir.ActivationFunctionType
AX_X = mybir.AxisListType.X

P = 128
GROUP = 4
MASKED = -(2.0 ** 53)
LN_EPS = 1e-5
LEAKY = 0.2
EXP_ROOM = 80.0
KEEP, FLOOR = 1e37, 1e-30

PE_LOOP = [
    ("v", 0), ("x1T", 0), ("qk", 0), ("qk", 1), ("x1T", 1), ("x1T", 2), ("h", 0), ("gate", 0), ("qk", 2),
    ("qk", 3), ("qwT", 0), ("h", 1), ("qk", 4), ("qk", 5), ("gate", 1), ("s", 0), ("wb", 0), ("qwT", 1),
    ("v", 1), ("wb", 1), ("wb", 2), ("pv1", 0), ("h", 2), ("wb", 3), ("pv1", 1), ("pv1", 2), ("x1T", 3),
    ("wb", 4), ("gate", 2), ("s", 1), ("pT", 0), ("pT", 1), ("pv1", 3), ("pv1", 4), ("wb", 5), ("h", 3),
    ("pv1", 5), ("s", 2), ("qwT", 2), ("pT", 2), ("pv0", 0), ("s", 3), ("pT", 3), ("wb", 6), ("v", 2),
    ("wb", 7), ("wb", 8), ("pv1", 6), ("pv0", 1), ("qwT", 3), ("f", 0), ("pT", 4), ("pv1", 7), ("pT", 5),
    ("pv1", 8), ("wb", 9), ("wb", 10), ("f", 1), ("pv0", 2), ("wb", 11), ("pv1", 9), ("v", 3), ("maskT", 0),
    ("pv1", 10), ("pT", 6), ("xT", 0), ("pv1", 11), ("pT", 7), ("f", 2), ("xT", 1), ("xT", 2), ("pv0", 3),
    ("gate", 3), ("xT", 3), ("f", 3), ("maskT", 1),
]
ACT_LOOP = [
    ("x1hi", 0), ("vout", 0), ("qkhi", 0), ("qkhi", 1), ("hout", 0), ("x1hi", 1), ("qkhi", 2), ("pqw", 0),
    ("qwhi", 0), ("qkhi", 3), ("hout", 1), ("qwTo", 0), ("gatet", 0), ("qkhi", 4), ("qkhi", 5), ("masks", 0),
    ("pqw", 1), ("qwhi", 1), ("x1hi", 2), ("qwTo", 1), ("vout", 1), ("exp", 0), ("hout", 2), ("x1hi", 3),
    ("gatet", 1), ("elu", 0), ("pTo", 0), ("exp", 1), ("pqw", 2), ("pTo", 1), ("qwhi", 2), ("hout", 3),
    ("qwTo", 2), ("chi", 0), ("pTo", 2), ("exp", 2), ("pTo", 3), ("vout", 2), ("pqw", 3), ("qwhi", 3),
    ("elu", 1), ("qwTo", 3), ("chi", 1), ("pTo", 4), ("pTo", 5), ("exp", 3), ("gatet", 2), ("chi", 2),
    ("elu", 2), ("pTo", 6), ("vout", 3), ("xhi", 0), ("pTo", 7), ("xhi", 1), ("xhi", 2), ("chi", 3), ("elu", 3),
    ("xhi", 3), ("gatet", 3),
]
DVE_LOOP = [
    ("x1lo", 0), ("qklo", 0), ("qklo", 1), ("gsum", 0), ("x1lo", 1), ("sd", 0), ("sda", 0), ("wlog", 0),
    ("qklo", 2), ("qwlo", 0), ("qklo", 3), ("qklo", 4), ("sd", 1), ("sda", 1), ("qklo", 5), ("wlog", 1),
    ("gsum", 1), ("qwlo", 1), ("x1lo", 2), ("e", 0), ("mask", 0), ("max", 0), ("e", 1), ("e", 2), ("rden0", 0),
    ("e", 3), ("e", 4), ("rden1", 0), ("f_raw", 0), ("x1lo", 3), ("sd", 2), ("mask", 1), ("max", 1), ("sda", 2),
    ("mixa", 0), ("e", 5), ("wlog", 2), ("mixb", 0), ("rden0", 1), ("sum1", 0), ("rden1", 1), ("stats1", 0),
    ("gsum", 2), ("mv1", 0), ("qwlo", 2), ("f_raw", 1), ("mask", 2), ("sd", 3), ("max", 2), ("clo", 0),
    ("sda", 3), ("mask", 3), ("e", 6), ("wlog", 3), ("rden0", 2), ("out", 0), ("e", 7), ("qwlo", 3), ("e", 8),
    ("max", 3), ("mixa", 1), ("sum0", 0), ("mixb", 1), ("stats0", 0), ("clo", 1), ("mv0", 0), ("sum1", 1),
    ("rden1", 2), ("stats1", 1), ("f_raw", 2), ("mv1", 1), ("e", 9), ("rden0", 3), ("e", 10), ("sum0", 1),
    ("e", 11), ("stats0", 1), ("clip", 0), ("mv0", 1), ("mixa", 2), ("clo", 2), ("x1", 0), ("mixb", 2),
    ("rden1", 3), ("xlo", 0), ("x1", 1), ("f_raw", 3), ("out", 1), ("sum0", 2), ("xlo", 1), ("stats0", 2),
    ("sum1", 2), ("clo", 3), ("stats1", 2), ("gsum", 3), ("xlo", 2), ("mv0", 2), ("mixa", 3), ("xlo", 3),
    ("mv1", 2), ("sum0", 3), ("mixb", 3), ("stats0", 3), ("sum1", 3), ("mv0", 3), ("stats1", 3), ("x1", 2),
    ("mv1", 3), ("x1", 3), ("clip", 1), ("out", 2), ("out", 3),
]
POOL_LOOP = [
    ("prod", 0), ("x_res", 0), ("prod", 1), ("rows", 0), ("rows", 1), ("norm", 0), ("prod", 2), ("fb", 0),
    ("ex", 0), ("norm", 1), ("prod", 3), ("rows", 2), ("fb", 1), ("rstd1", 0), ("norm", 2), ("ex", 1),
    ("rows", 3), ("rstd0", 0), ("fb", 2), ("norm", 3), ("ex", 2), ("rstd1", 1), ("rstd0", 1), ("fb", 3),
    ("ex", 3), ("rstd1", 2), ("rstd0", 2), ("rstd0", 3), ("rstd1", 3),
]
PE_FIRST = [
    ("qk", 0), ("qk", 1), ("qk", 2), ("qk", 3), ("maskT", 0), ("qk", 4), ("qk", 5), ("ob", 0), ("s", 0),
    ("v", 0), ("s", 1), ("v", 1), ("gT", 0), ("s", 2), ("pT", 0), ("pT", 1), ("v", 2), ("pv0", 0), ("s", 3),
    ("pT", 2), ("pT", 3), ("f", 0), ("pT", 4), ("pT", 5), ("pv0", 1), ("v", 3), ("f", 1), ("xT", 0), ("pv0", 2),
    ("maskT", 1), ("gT", 1), ("pT", 6), ("pT", 7), ("f", 2), ("pv0", 3), ("gT", 2), ("xT", 1), ("xT", 2),
    ("f", 3), ("xT", 3),
]
ACT_FIRST = [
    ("masks", 0), ("whi", 2), ("qkhi", 0), ("qkhi", 1), ("whi", 3), ("qkhi", 2), ("qkhi", 3), ("qkhi", 4),
    ("whi", 4), ("qkhi", 5), ("vout", 0), ("exp", 0), ("exp", 1), ("pTo", 0), ("vout", 1), ("pTo", 1),
    ("exp", 2), ("chi", 0), ("pTo", 2), ("ghi", 0), ("pTo", 3), ("vout", 2), ("pTo", 4), ("chi", 1), ("exp", 3),
    ("pTo", 5), ("vout", 3), ("xhi", 0), ("chi", 2), ("pTo", 6), ("pTo", 7), ("ghi", 1), ("chi", 3), ("xhi", 1),
    ("xhi", 2), ("ghi", 2), ("xhi", 3),
]
DVE_FIRST = [
    ("qklo", 0), ("qklo", 1), ("consts", 0), ("qklo", 2), ("qklo", 3), ("wlo", 2), ("qklo", 4), ("wlo", 3),
    ("qklo", 5), ("outb", 0), ("mask", 0), ("max", 0), ("mask", 1), ("rden0", 0), ("max", 1), ("clip", 0),
    ("mask", 2), ("rden0", 1), ("max", 2), ("clo", 0), ("rden0", 2), ("glo", 0), ("mask", 3), ("max", 3),
    ("sum0", 0), ("clo", 1), ("wlo", 4), ("stats0", 0), ("rden0", 3), ("sum0", 1), ("mv0", 0), ("xlo", 0),
    ("clip", 1), ("clo", 2), ("stats0", 1), ("mv0", 1), ("x1", 0), ("glo", 1), ("sum0", 2), ("x1", 1),
    ("stats0", 2), ("clo", 3), ("xlo", 1), ("xlo", 2), ("glo", 2), ("mv0", 2), ("sum0", 3), ("stats0", 3),
    ("mv0", 3), ("x1", 2), ("xlo", 3), ("x1", 3),
]
POOL_FIRST = [
    ("x_res", 0), ("norm", 0), ("norm", 1), ("norm", 2), ("norm", 3), ("rstd0", 0), ("rstd0", 1), ("rstd0", 2),
    ("rstd0", 3),
]
PE_LAST = [
    ("x1T", 0), ("x1T", 1), ("h", 0), ("gate", 0), ("x1T", 2), ("h", 1), ("qwT", 0), ("gate", 1), ("wb", 0),
    ("wb", 1), ("h", 2), ("pv1", 0), ("qwT", 1), ("wb", 2), ("pv1", 1), ("pv1", 2), ("wb", 3), ("wb", 4),
    ("gate", 2), ("wb", 5), ("x1T", 3), ("pv1", 3), ("pv1", 4), ("qwT", 2), ("pv1", 5), ("h", 3), ("wb", 6),
    ("wb", 7), ("pv1", 6), ("wb", 8), ("qwT", 3), ("pv1", 7), ("pv1", 8), ("wb", 9), ("wb", 10), ("pv1", 9),
    ("wb", 11), ("pv1", 10), ("pv1", 11), ("gate", 3),
]
ACT_LAST = [
    ("x1hi", 0), ("hout", 0), ("x1hi", 1), ("pqw", 0), ("qwhi", 0), ("qwTo", 0), ("hout", 1), ("x1hi", 2),
    ("pqw", 1), ("qwhi", 1), ("gatet", 0), ("qwTo", 1), ("gatet", 1), ("hout", 2), ("pqw", 2), ("x1hi", 3),
    ("elu", 0), ("qwhi", 2), ("qwTo", 2), ("hout", 3), ("elu", 1), ("pqw", 3), ("qwhi", 3), ("qwTo", 3),
    ("elu", 2), ("gatet", 2), ("elu", 3), ("gatet", 3),
]
DVE_LAST = [
    ("x1lo", 0), ("x1lo", 1), ("sd", 0), ("sda", 0), ("wlog", 0), ("gsum", 0), ("qwlo", 0), ("x1lo", 2),
    ("e", 0), ("sd", 1), ("sda", 1), ("wlog", 1), ("qwlo", 1), ("e", 1), ("gsum", 1), ("e", 2), ("e", 3),
    ("e", 4), ("rden1", 0), ("f_raw", 0), ("sd", 2), ("sda", 2), ("wlog", 2), ("x1lo", 3), ("e", 5),
    ("qwlo", 2), ("mixa", 0), ("rden1", 1), ("mixb", 0), ("sum1", 0), ("stats1", 0), ("f_raw", 1), ("e", 6),
    ("e", 7), ("sd", 3), ("mv1", 0), ("sda", 3), ("wlog", 3), ("qwlo", 3), ("e", 8), ("mixa", 1), ("mixb", 1),
    ("sum1", 1), ("gsum", 2), ("stats1", 1), ("rden1", 2), ("f_raw", 2), ("e", 9), ("e", 10), ("out", 0),
    ("e", 11), ("mv1", 1), ("mixa", 2), ("rden1", 3), ("f_raw", 3), ("mixb", 2), ("out", 1), ("sum1", 2),
    ("gsum", 3), ("stats1", 2), ("mv1", 2), ("mixa", 3), ("mixb", 3), ("sum1", 3), ("stats1", 3), ("mv1", 3),
    ("out", 2), ("out", 3),
]
POOL_LAST = [
    ("prod", 0), ("rows", 0), ("prod", 1), ("rows", 1), ("prod", 2), ("fb", 0), ("ex", 0), ("rows", 2),
    ("fb", 1), ("prod", 3), ("ex", 1), ("rows", 3), ("rstd1", 0), ("fb", 2), ("ex", 2), ("rstd1", 1), ("fb", 3),
    ("ex", 3), ("rstd1", 2), ("rstd1", 3),
]
ORDERS = {
    "load": {"PE": [("xT", g) for g in range(GROUP)],
             "ACT": [("whi", 0)] + [("xhi", g) for g in range(GROUP)] + [("whi", 1)],
             "DVE": [("wlo", 0)] + [("xlo", g) for g in range(GROUP)] + [("wlo", 1)],
             "POOL": []},
    "first": {"PE": PE_FIRST, "ACT": ACT_FIRST, "DVE": DVE_FIRST, "POOL": POOL_FIRST},
    "loop": {"PE": PE_LOOP, "ACT": ACT_LOOP, "DVE": DVE_LOOP, "POOL": POOL_LOOP},
    "last": {"PE": PE_LAST, "ACT": ACT_LAST, "DVE": DVE_LAST, "POOL": POOL_LAST},
}
ORDERS["second"] = ORDERS["loop"]
ORDERS["drain"] = {e: [(n, k) for n, k in steps if n not in ("xT", "xhi", "xlo")] for e, steps in ORDERS["loop"].items()}
BEFORE = {"first": "load", "second": "first", "loop": "second", "drain": "loop", "last": "drain"}
WEIGHTS = ("q", "k", "v", "f", "h")
SHIFT = {n: 2 for n in ("xT", "xhi", "xlo")} | {n: 1 for n in (
    "qk", "s", "v", "norm", "pT", "pTo", "pv0", "f", "maskT", "masks", "qkhi", "vout", "exp", "chi", "qklo", "mask",
    "max", "rden0", "clo", "sum0", "stats0", "mv0", "x1", "clip", "x_res", "rstd0")}


def upto(group, per, k):
    return group * per + k


def bass_graph_transformer_gat(nc, x, adj, Wq, bq, Wk, bk, Wv, bv, Wf, bf, W1, b1, w_src, w_dst, H_w, H_b, out):
    graphs, nodes, D = x.shape
    NG = graphs // GROUP
    KT = D // P
    H0, HD0 = 6, 64
    H1, _, HD1 = W1.shape
    PAIRS = H0 // 2
    GN = GROUP * P
    SCALE = float(HD0) ** -0.5
    HI, LO = 0, 1
    BLOCK = 32
    QW_ROWS = 3 * BLOCK
    THIRDS = 3
    THREE = ((HI, HI), (HI, LO), (LO, HI))
    assert nodes == P and KT * P == D and H0 * HD0 == D and H1 * HD1 == D

    with ExitStack() as ctx:
        def sb(name, shape, dt=F32):
            return ctx.enter_context(nc.sbuf_tensor(name, shape, dt))

        def psum(name, shape, dt=F32):
            return ctx.enter_context(nc.psum_tensor(name, shape, dt))

        def sem(name):
            return ctx.enter_context(nc.semaphore(name))

        t_bank = [psum(f"t_bank{i}", [P, 512]) for i in range(2)]
        p_bank = [psum(f"p_bank{i}", [P, 512]) for i in range(2)]
        scores = psum("scores", [P, 2, 512])
        context0 = psum("context0", [P, 512])
        context1 = psum("context1", [P, 512])

        names = ("q", "k", "v", "f", "h", "g")
        w = {n: sb(f"w_{n}", [P, 2, KT, D], F32R) for n in names}
        ident = sb("ident", [P, P])
        ident_b = sb("ident_b", [P, P], BF16)
        bias_q = sb("bias_q", [P, 2, PAIRS])
        bias_v = sb("bias_v", [P, KT])
        bias_f = sb("bias_f", [P, D])
        out_bias = sb("out_bias", [P, D])
        bias_1 = sb("bias_1", [P, HD1])
        w_sd = sb("w_sd", [P, 2, D])
        sd_shift = sb("sd_shift", [P, 2, H1])
        gate_bias = sb("gate_bias", [P, D])
        eps0 = sb("eps0", [P, 1])
        eps1 = sb("eps1", [P, 1])
        minus_half = sb("minus_half", [P, 1])
        minus_one = sb("minus_one", [P, 1])

        x_in = sb("x_in", [P, GROUP, D])
        x_res = sb("x_res", [P, GROUP, D])
        adj_in = sb("adj_in", [P, GROUP, P], U8)
        adj_b = sb("adj_b", [P, GROUP, P], BF16)
        neg = sb("neg", [P, GROUP, P], BF16)
        xT = sb("xT", [P, 2, KT, GN], F32R)
        qT = sb("qT", [P, 2, PAIRS, GN], F32R)
        kT = sb("kT", [P, 2, PAIRS, GN], F32R)
        v = sb("v", [P, GROUP, D])
        masked = sb("masked", [P, 2, H0, P])
        neg_max = sb("neg_max", [P, H0])
        probs0 = sb("probs0", [P, 2, 2, PAIRS * P])
        probs0T = sb("probs0T", [P, 2, 2, PAIRS * P])
        den0 = sb("den0", [P, 2, H0])
        rden0 = sb("rden0", [P, H0])
        cT = sb("cT", [P, 2, KT, P], F32R)
        sum0 = sb("sum0", [P, 2, D])
        stats0 = sb("stats0", [P, GROUP, 6])
        mv0 = sb("mv0", [P, GROUP, 2])
        ve0 = sb("ve0", [P, GROUP])
        rstd0 = sb("rstd0", [P, GROUP])
        x1 = sb("x1", [P, GROUP, D])
        clip = sb("clip", [P, GROUP, P])
        x1T = sb("x1T", [P, 2, KT, P], F32R)
        th = sb("th", [P, D])
        h = sb("h", [P, 2, H1, HD1 + 1])
        gate_sum = sb("gate_sum", [P, D])
        gate_t = sb("gate_t", [P, 2, D])
        prod = sb("prod", [P, 2, D])
        sd = sb("sd", [P, 2, H1])
        sda = sb("sda", [P, 2, H1])
        wlog = sb("wlog", [P, H1])
        pqw = sb("pqw", [P, 2, 3, H1])
        qw_parts = sb("qw_parts", [P, 2, 2, QW_ROWS], F32R)
        qwT = sb("qwT", [QW_ROWS, 2, 2, P], F32R)
        own_head = sb("own_head", [QW_ROWS, H1])
        w_rows = sb("w_rows", [P, 2, H1, P], F32R)
        weights = sb("weights", [P, H1, P])
        rden1 = sb("rden1", [P, H1])
        f_raw = sb("f_raw", [P, D])
        f_b = sb("f_b", [P, 2, D])
        elu_steps = sb("elu_steps", [P, 3, D])
        f_neg, f_exp, exp_less_x = (elu_steps[:, i, :] for i in range(3))
        mix = sb("mix", [P, D])
        sum1 = sb("sum1", [P, 2, D])
        stats1 = sb("stats1", [P, GROUP, 6])
        mv1 = sb("mv1", [P, GROUP, 2])
        ve1 = sb("ve1", [P, GROUP])
        rstd1 = sb("rstd1", [P, GROUP])
        y_out = sb("y_out", [P, 2, D])
        stage_ap = {
            "q": probs0T[:].rearrange("p a b c -> p (a b c)")[:, 0:KT * D],
            "k": weights[:].rearrange("p h i -> p (h i)")[:, 0:KT * D],
            "v": x_res[:].rearrange("p g d -> p (g d)")[:, 0:KT * D],
            "f": probs0[:].rearrange("p a b c -> p (a b c)")[:, 0:KT * D],
            "h": x1[:].rearrange("p g d -> p (g d)")[:, 0:KT * D],
        }
        stage_ap["g"] = elu_steps[:].rearrange("p k n -> p (k n)")
        stage_ap = {n: a.rearrange("p (k n) -> p k n", k=KT) for n, a in stage_ap.items()}
        dmas = {n: sem(f"w_{n}_loaded") for n in names}

        s_const = sem("const_made")
        s_copies = sem("ident_copied")
        s_scaled = sem("bias_q_scaled")
        s_table = sem("table_loaded")
        s_head = sem("own_head_made")
        s_bias_qk = sem("bias_qk_loaded")
        s_bias_vf = sem("bias_vf_loaded")
        s_bias1 = sem("layer1_biases_loaded")
        s_whi = sem("w_hi_made")
        s_wlo = sem("w_lo_made")
        s_gT = sem("g_transposed")
        s_ghi = sem("g_hi_made")
        s_glo = sem("g_lo_made")
        s_ob = sem("out_bias_summed")
        s_outb = sem("out_bias_made")
        s_shift = sem("sd_shift_steps")
        s_consts = sem("constants_made")
        s_free = sem("inputs_free")
        s_x = sem("x_loaded")
        s_adj = sem("adj_loaded")
        s_store = [sem(f"stored{i}") for i in range(2)]
        pe = {n: sem(f"pe_{n}") for n in ("xT", "qk", "s", "v", "pT", "pv0", "f", "maskT",
                                           "x1T", "h", "gate", "qwT", "wb", "pv1")}
        s_neg = sem("neg_made")
        s_adjb = sem("adj_b_made")
        s_xhi = sem("x_hi_made")
        s_qkhi = sem("qk_hi_made")
        s_v = sem("v_copied")
        s_exp = sem("probs0_made")
        s_pT = sem("probs0T_copied")
        s_chi = sem("c_hi_made")
        s_x1hi = sem("x1_hi_made")
        s_th = sem("th_made")
        s_h = sem("h_copied")
        s_gsum = sem("gate_sum_made")
        s_gate = sem("gate_made")
        s_pqw = sem("pqw_made")
        s_qwhi = sem("qw_hi_made")
        s_qwT = sem("qwT_copied")
        s_fneg = sem("f_neg_made")
        s_elu = sem("f_exp_made")
        s_xlo = sem("x_lo_made")
        s_qklo = sem("qk_lo_made")
        s_masked = sem("scores_masked")
        s_max = sem("max_found")
        s_rden0 = sem("rden0_made")
        s_clo = sem("c_lo_made")
        s_sum0 = sem("sum0_made")
        s_st0 = sem("stats0_made")
        s_seen = sem("stats_seen")
        s_mv0 = sem("mv0_made")
        s_x1 = sem("x1_made")
        s_mx = sem("clip_made")
        s_x1lo = sem("x1_lo_made")
        s_sd = sem("sd_made")
        s_sda = sem("sd_shifted")
        s_wlog = sem("w_exponent_made")
        s_qwlo = sem("qw_lo_made")
        s_e = sem("weights_clipped")
        s_rden1 = sem("rden1_made")
        s_fraw = sem("f_made")
        s_mixa = sem("mixa_made")
        s_mixb = sem("mixb_made")
        s_sum1 = sem("sum1_made")
        s_st1 = sem("stats1_made")
        s_mv1 = sem("mv1_made")
        s_y = sem("y_made")
        s_xb = sem("x_res_made")
        s_ve0 = sem("var_eps0_made")
        s_rstd0 = sem("rstd0_made")
        s_norm = sem("probs0_normalized")
        s_rows = sem("w_rows_made")
        s_cleared = sem("qw_parts_cleared")
        s_prod = sem("prod_made")
        s_fb = sem("f_b_made")
        s_ex = sem("exp_less_x_made")
        s_ve1 = sem("var_eps1_made")
        s_rstd1 = sem("rstd1_made")

        x_dram = x.rearrange("g p d -> p g d")
        out_dram = out.rearrange("g p d -> p g d")
        adj_dram = adj.rearrange("g p m -> p g m")

        def wait(eng, s, n):
            if not isinstance(n, int) or n > 0:
                eng.wait_ge(s, n)

        def phases(eng, step, engine):
            for name, k in ORDERS["load"][engine]:
                step(name, k, -2, "load")
            for name, k in ORDERS["first"][engine]:
                step(name, k, -1, "first")
            for name, k in ORDERS["loop"][engine]:
                step(name, k, 0, "second")
            with eng.Fori(1, NG - 2) as u:
                for name, k in ORDERS["loop"][engine]:
                    step(name, k, u, "loop")
            for name, k in ORDERS["drain"][engine]:
                step(name, k, NG - 2, "drain")
            for name, k in ORDERS["last"][engine]:
                step(name, k, NG - 1, "last")

        def over_heads(ap, n):
            return ap.unsqueeze(1).broadcast_to([ap.shape[0], n, ap.shape[-1]])

        def per_head(ap, n):
            return ap.unsqueeze(2).broadcast_to([ap.shape[0], ap.shape[-1], n])

        block = ctx.enter_context(nc.Block())

        @block.sync
        def _(sp):
            sp.dma_start(x_in[:], x_dram[:, 0:GROUP, :]).then_inc(s_x, 16)
            for n, src in (("q", Wq), ("k", Wk)):
                sp.dma_start(stage_ap[n], src.rearrange("(k p) n -> p k n", p=P)).then_inc(dmas[n], 16)
            for n, src in ((0, bq), (1, bk)):
                sp.dma_start(bias_q[:, n, :], src.rearrange("(m p) -> p m", p=P),
                             allow_slow_non_contiguous=True).then_inc(s_bias_qk, 16)
            sp.dma_start(adj_in[:], adj_dram[:, 0:GROUP, :]).then_inc(s_adj, 16)
            for n, src in (("v", Wv), ("f", Wf)):
                sp.dma_start(stage_ap[n], src.rearrange("(k p) n -> p k n", p=P)).then_inc(dmas[n], 16)
            sp.dma_start(bias_v[:], bv.rearrange("(m p) -> p m", p=P),
                         allow_slow_non_contiguous=True).then_inc(s_bias_vf, 16)
            sp.dma_start(bias_f[:], bf.partition_broadcast(P)).then_inc(s_bias_vf, 16)
            for kt in range(KT):
                sp.dma_start(stage_ap["h"][:, kt, :].rearrange("p (a e) -> p a e", a=H1),
                             W1[:, kt * P:(kt + 1) * P, :].rearrange("a p e -> p a e")).then_inc(dmas["h"], 16)
            sp.dma_start(stage_ap["g"], H_w.rearrange("(k p) n -> p k n", p=P)).then_inc(dmas["g"], 16)
            sp.dma_start(bias_1[:], b1.partition_broadcast(P)).then_inc(s_bias1, 16)
            sp.dma_start(gate_bias[:], H_b.partition_broadcast(P)).then_inc(s_bias1, 16)
            for n, src in ((0, w_src), (1, w_dst)):
                sp.dma_start(w_sd[:, n, :],
                             src.rearrange("a e o -> (a e o)").partition_broadcast(P)).then_inc(s_bias1, 16)

            def at(n):
                return n if isinstance(n, int) else sp.snap(n)

            def load(t):
                first = at(t * GROUP)
                sp.wait_ge(pe["xT"], upto(t, GROUP, 0))
                sp.wait_ge(s_xb, upto(t, 1, 0))
                sp.wait_ge(s_adjb, upto(t, 1, 0))
                sp.sem_inc(s_free, 1)
                sp.dma_start(x_in[:], x_dram[:, bass.ds(first, GROUP), :]).then_inc(s_x, 16)
                sp.dma_start(adj_in[:], adj_dram[:, bass.ds(first, GROUP), :]).then_inc(s_adj, 16)

            def store(t):
                for g in range(GROUP):
                    graph = at(t * GROUP + g)
                    sp.wait_ge(s_y, upto(t, GROUP, g + 1))
                    sp.dma_start(out_dram[:, bass.ds(graph, 1), :],
                                 y_out[:, g % 2, :].unsqueeze(1)).then_inc(s_store[g % 2], 16)

            load(1)
            load(2)
            store(0)
            with sp.Fori(1, NG - 2) as u:
                load(u + 2)
                store(u)
            store(NG - 2)
            store(NG - 1)
            for g in range(2):
                sp.wait_ge(s_store[g], graphs // 2 * 16)

        @block.tensor
        def _(te):
            te.wait_ge(s_const, 4)
            te.wait_ge(s_copies, 1)

            t_freed = {"xT": (s_xlo, GROUP), "x1T": (s_x1lo, GROUP),
                       "qwT": (s_qwT, GROUP), "wb": (s_e, THIRDS * GROUP), "maskT": (s_mx, 2), "pT": (s_pT, 2 * GROUP)}
            p_freed = {"qk": (s_qklo, 2 * PAIRS), "v": (s_v, GROUP), "f": (s_sum0, GROUP),
                       "h": (s_h, GROUP), "gate": (s_gsum, GROUP)}

            def bank(banks, freed, name, k, g1, phase):
                order = bank_uses(freed, phase)
                at = order.index((name, k))
                back = 0
                if at < 2 and phase in BEFORE:
                    order, back = bank_uses(freed, BEFORE[phase]), 1
                if at >= 2 or back and order:
                    before, kb = order[at - 2]
                    s, per = freed[before]
                    wait(te, s, upto(g1 + SHIFT.get(before, 0) - back, per, kb + 1))
                return banks[at % 2]

            def project(dst, left, right):
                n = 0
                for kt in range(KT):
                    for a, b in THREE:
                        last = te.matmul(dst, left(a, kt), right(b, kt), start=(n == 0), stop=(n == 3 * KT - 1))
                        n += 1
                return last

            def head(ap, part, j, b, g):
                return ap[b * HD0:(b + 1) * HD0, part, j, g * P:(g + 1) * P]

            def step(name, k, g1, phase):
                g0, gx = g1 + 1, g1 + 2
                if name == "ob":
                    te.wait_ge(s_bias_vf, 2 * 16)
                    te.wait_ge(dmas["f"], 16)
                    for kt in range(KT):
                        last = te.matmul(context1[:, 0:D], bias_v[:, kt:kt + 1].broadcast_to([P, P]),
                                         stage_ap["f"][:, kt, :], start=(kt == 0), stop=(kt == KT - 1))
                    last.then_inc(s_ob, 1)
                elif name == "gT":
                    te.wait_ge(dmas["g"], 16)
                    te.wait_ge(s_outb, 1)
                    wait(te, s_glo, k)
                    for ot in range(KT):
                        last = te.transpose(context1[:, ot * P:(ot + 1) * P],
                                            stage_ap["g"][:, ot, k * P:(k + 1) * P], ident[:])
                    last.then_inc(s_gT, 1)
                elif name == "xT":
                    if k == 0:
                        te.wait_ge(s_x, upto(gx, 16, 16))
                    dst = bank(t_bank, t_freed, name, k, g1, phase)
                    for kt in range(KT):
                        last = te.transpose(dst[:, kt * P:(kt + 1) * P], x_in[:, k, kt * P:(kt + 1) * P], ident[:])
                    last.then_inc(pe["xT"], 1)
                elif name == "qk":
                    if phase == "first" and k == 0:
                        te.wait_ge(s_wlo, 2)
                    if k == 0:
                        te.wait_ge(s_xlo, upto(g0, GROUP, GROUP))
                    dst = bank(p_bank, p_freed, name, k, g1, phase)
                    j, m = k // 2, w["qk"[k % 2]]
                    project(dst[:, :], lambda a, kt: m[:, a, kt, j * P:(j + 1) * P],
                            lambda b, kt: xT[:, b, kt, :]).then_inc(pe["qk"], 1)
                elif name == "v":
                    if phase == "first" and k == 0:
                        te.wait_ge(s_wlo, 3)
                    dst = bank(p_bank, p_freed, name, k, g1, phase)
                    project(dst[:, 0:D], lambda a, kt: xT[:, a, kt, k * P:(k + 1) * P],
                            lambda b, kt: w["v"][:, b, kt, :]).then_inc(pe["v"], 1)
                elif name == "s":
                    if k == 0:
                        te.wait_ge(s_qklo, upto(g0, 2 * PAIRS, 2 * PAIRS))
                    wait(te, s_masked, upto(g0, GROUP, k))
                    for j in range(PAIRS):
                        for a, c in THREE:
                            for b in range(2):
                                last = te.matmul(scores[:, b, j * P:(j + 1) * P], head(qT, a, j, b, k),
                                                 head(kT, c, j, b, k), start=((a, c) == THREE[0]),
                                                 stop=((a, c) == THREE[-1]))
                    last.then_inc(pe["s"], 1)
                elif name == "pT":
                    g, b = divmod(k, 2)
                    te.wait_ge(s_norm, upto(g0, GROUP, g + 1))
                    dst = bank(t_bank, t_freed, name, k, g1, phase)
                    for j in range(PAIRS):
                        last = te.transpose(dst[:, j * P:(j + 1) * P], probs0[:, g % 2, b, j * P:(j + 1) * P], ident[:])
                    last.then_inc(pe["pT"], 1)
                elif name == "pv0":
                    te.wait_ge(s_pT, upto(g0, 2 * GROUP, 2 * k + 2))
                    te.wait_ge(s_v, upto(g0, GROUP, k + 1))
                    wait(te, s_clo, upto(g0, GROUP, k))
                    for j in range(PAIRS):
                        for b in range(2):
                            n = 2 * j + b
                            last = te.matmul(context0[b * HD0:(b + 1) * HD0, j * P:(j + 1) * P],
                                             v[:, k, n * HD0:(n + 1) * HD0],
                                             probs0T[:, k % 2, b, j * P:(j + 1) * P], start=True, stop=True)
                    last.then_inc(pe["pv0"], 1)
                elif name == "f":
                    te.wait_ge(s_clo, upto(g0, GROUP, k + 1))
                    if phase == "first" and k == 0:
                        te.wait_ge(s_wlo, 4)
                    dst = bank(p_bank, p_freed, name, k, g1, phase)
                    project(dst[:, 0:D], lambda a, kt: cT[:, a, kt, :],
                            lambda b, kt: w["f"][:, b, kt, :]).then_inc(pe["f"], 1)
                elif name == "maskT":
                    dst = bank(t_bank, t_freed, name, k, g1, phase)
                    if k == 0:
                        te.wait_ge(s_adjb, upto(g0, 1, 1))
                    for i in range(2):
                        last = te.transpose(dst[:, 0:P].bitcast(BF16)[:, i * P:(i + 1) * P],
                                            adj_b[:, 2 * k + i, :], ident_b[:])
                    last.then_inc(pe["maskT"], 1)
                elif name == "x1T":
                    te.wait_ge(s_x1, upto(g1, GROUP, k + 1))
                    dst = bank(t_bank, t_freed, name, k, g1, phase)
                    for kt in range(KT):
                        last = te.transpose(dst[:, kt * P:(kt + 1) * P], x1[:, k, kt * P:(kt + 1) * P], ident[:])
                    last.then_inc(pe["x1T"], 1)
                elif name == "h":
                    if phase == "second" and k == 0:
                        te.wait_ge(s_wlo, 5)
                        te.wait_ge(s_glo, KT)
                    te.wait_ge(s_x1lo, upto(g1, GROUP, k + 1))
                    dst = bank(p_bank, p_freed, name, k, g1, phase)
                    project(dst[:, 0:D], lambda a, kt: x1T[:, a, kt, :],
                            lambda b, kt: w["h"][:, b, kt, :]).then_inc(pe["h"], 1)
                elif name == "gate":
                    dst = bank(p_bank, p_freed, name, k, g1, phase)
                    project(dst[:, 0:D], lambda a, kt: x1T[:, a, kt, :],
                            lambda b, kt: w["g"][:, b, kt, :]).then_inc(pe["gate"], 1)
                elif name == "qwT":
                    te.wait_ge(s_qwlo, upto(g1, GROUP, k + 1))
                    dst = bank(t_bank, t_freed, name, k, g1, phase)
                    for i in range(2):
                        last = te.transpose(dst[0:QW_ROWS, i * P:(i + 1) * P], qw_parts[:, k % 2, i, :].bitcast(F32),
                                            ident[:])
                    last.then_inc(pe["qwT"], 1)
                elif name == "wb":
                    g, r = divmod(k, THIRDS)
                    te.wait_ge(s_rows, upto(g1, GROUP, g + 1))
                    dst = bank(t_bank, t_freed, name, k, g1, phase)
                    heads = slice(H1 // THIRDS * r, H1 // THIRDS * (r + 1))
                    te.matmul(dst[:, :], qwT[:, g % 2, 0, :],
                              w_rows[0:QW_ROWS, g % 2, heads, :].rearrange("p h i -> p (h i)"),
                              start=True, stop=True).then_inc(pe["wb"], 1)
                elif name == "pv1":
                    g, r = divmod(k, THIRDS)
                    te.wait_ge(s_e, upto(g1, THIRDS * GROUP, k + 1))
                    te.wait_ge(s_h, upto(g1, GROUP, g + 1))
                    wait(te, s_fraw, upto(g1, GROUP, g))
                    for n in range(H1 // THIRDS * r, H1 // THIRDS * (r + 1)):
                        last = te.matmul(context1[:, n * (HD1 + 1):(n + 1) * (HD1 + 1)], weights[:, n, :],
                                         h[:, g % 2, n, :], start=True, stop=True)
                    last.then_inc(pe["pv1"], 1)

            phases(te, step, "PE")

        @block.scalar
        def _(act):
            act.wait_ge(s_const, 4)
            act.activation(ve0[:, 0:1], minus_half[:], ACT.Exp).then_inc(s_table, 1)
            act.activation(ident_b[:], ident[:], ACT.Copy).then_inc(s_copies, 1)

            def step(name, k, g1, phase):
                g0, gx = g1 + 1, g1 + 2
                if name == "whi":
                    n = WEIGHTS[k]
                    act.wait_ge(dmas[n], 16 * KT if n == "h" else 16)
                    act.activation(w[n][:, HI], stage_ap[n], ACT.Copy,
                                   scale=SCALE if n == "q" else 1.0).then_inc(s_whi, 1)
                elif name == "ghi":
                    act.wait_ge(s_gT, k + 1)
                    act.activation(w["g"][:, HI, k, :], context1[:, 0:D], ACT.Copy).then_inc(s_ghi, 1)
                elif name == "masks":
                    act.wait_ge(s_adj, upto(g0, 16, 16))
                    wait(act, s_masked, upto(g0, GROUP, 0))
                    act.activation(neg[:], adj_in[:], ACT.Copy, scale=-MASKED, bias=MASKED).then_inc(s_neg, 1)
                    wait(act, pe["maskT"], upto(g0, 2, 0))
                    act.activation(adj_b[:], adj_in[:], ACT.Copy).then_inc(s_adjb, 1)
                elif name == "xhi":
                    act.wait_ge(pe["xT"], upto(gx, GROUP, k + 1))
                    if k == 0:
                        wait(act, pe["v"], upto(gx, GROUP, 0))
                        wait(act, pe["qk"], upto(gx, 2 * PAIRS, 0))
                    act.activation(xT[:, HI, :, k * P:(k + 1) * P],
                                   t_bank[t_at("xT", k, phase)][:, 0:D].rearrange("p (k n) -> p k n", k=KT),
                                   ACT.Copy).then_inc(s_xhi, 1)
                elif name == "qkhi":
                    act.wait_ge(pe["qk"], upto(g0, 2 * PAIRS, k + 1))
                    if k == 0:
                        wait(act, pe["s"], upto(g0, GROUP, 0))
                    if phase == "first" and k == 0:
                        act.wait_ge(s_bias_qk, 2 * 16)
                        act.activation(bias_q[:, 0, :], bias_q[:, 0, :], ACT.Copy, scale=SCALE).then_inc(s_scaled, 1)
                        act.wait_ge(s_scaled, 1)
                    dst = (qT, kT)[k % 2]
                    act.activation(dst[:, HI, k // 2, :], p_bank[p_at("qk", k, phase)][:, :], ACT.Identity,
                                   bias=bias_q[:, k % 2, k // 2:k // 2 + 1]).then_inc(s_qkhi, 1)
                elif name == "vout":
                    act.wait_ge(pe["v"], upto(g0, GROUP, k + 1))
                    wait(act, pe["pv0"], upto(g0, GROUP, k + 1 - GROUP))
                    act.activation(v[:, k, :], p_bank[p_at("v", k, phase)][:, 0:D], ACT.Copy).then_inc(s_v, 1)
                elif name == "exp":
                    act.wait_ge(s_max, upto(g0, GROUP, k + 1))
                    wait(act, pe["pT"], upto(g0, 2 * GROUP, 2 * (k - 1)))
                    if phase == "first" and k == 0:
                        act.wait_ge(s_wlo, 4)
                        act.wait_ge(s_ob, 1)
                    for b in range(2):
                        for j in range(PAIRS):
                            last = act.activation(probs0[:, k % 2, b, j * P:(j + 1) * P], masked[:, k % 2, b * PAIRS + j, :],
                                                  ACT.Exp, bias=neg_max[:, b * PAIRS + j:b * PAIRS + j + 1],
                                                  accum_out=den0[:, k % 2, b * PAIRS + j:b * PAIRS + j + 1])
                    last.then_inc(s_exp, 1)
                elif name == "pTo":
                    g, b = divmod(k, 2)
                    act.wait_ge(pe["pT"], upto(g0, 2 * GROUP, k + 1))
                    wait(act, pe["pv0"], upto(g0, GROUP, g - 1))
                    act.activation(probs0T[:, g % 2, b, :], t_bank[t_at("pT", k, phase)][:, 0:PAIRS * P],
                                   ACT.Copy).then_inc(s_pT, 1)
                elif name == "chi":
                    act.wait_ge(pe["pv0"], upto(g0, GROUP, k + 1))
                    wait(act, pe["f"], upto(g0, GROUP, k))
                    act.activation(cT[:, HI], context0[:, 0:D].rearrange("p (k n) -> p k n", k=KT),
                                   ACT.Copy).then_inc(s_chi, 1)
                elif name == "x1hi":
                    act.wait_ge(pe["x1T"], upto(g1, GROUP, k + 1))
                    wait(act, pe["gate"], upto(g1, GROUP, k))
                    act.activation(x1T[:, HI], t_bank[t_at("x1T", k, phase)][:, 0:D].rearrange("p (k n) -> p k n", k=KT),
                                   ACT.Copy).then_inc(s_x1hi, 1)
                elif name == "hout":
                    src = p_bank[p_at("h", k, phase)][:, 0:D]
                    act.wait_ge(pe["h"], upto(g1, GROUP, k + 1))
                    wait(act, s_prod, upto(g1, GROUP, k))
                    act.activation(th[:], src, ACT.Tanh).then_inc(s_th, 1)
                    wait(act, pe["pv1"], upto(g1, THIRDS * GROUP, THIRDS * (k - 1)))
                    act.activation(h[:, k % 2, :, 0:HD1], src.rearrange("p (h e) -> p h e", h=H1),
                                   ACT.Copy).then_inc(s_h, 1)
                elif name == "gatet":
                    act.wait_ge(s_gsum, upto(g1, GROUP, k + 1))
                    wait(act, s_sum1, upto(g1, GROUP, k - 1))
                    act.activation(gate_t[:, k % 2, :], gate_sum[:], ACT.Tanh, scale=0.5).then_inc(s_gate, 1)
                elif name == "pqw":
                    act.wait_ge(s_sda, upto(g1, GROUP, k + 1))
                    wait(act, s_e, upto(g1, THIRDS * GROUP, THIRDS * (k - 1)))
                    wait(act, s_qwlo, upto(g1, GROUP, k - 1))
                    act.activation(pqw[:, k % 2, 0, :], sda[:, 1, :], ACT.Exp).then_inc(s_pqw, 1)
                    act.activation(pqw[:, k % 2, 1, :], sda[:, 1, :], ACT.Exp, scale=LEAKY).then_inc(s_pqw, 1)
                    act.wait_ge(s_wlog, upto(g1, GROUP, k + 1))
                    act.activation(pqw[:, k % 2, 2, :], wlog[:], ACT.Exp, scale=LEAKY - 1.0).then_inc(s_pqw, 1)
                elif name == "qwhi":
                    act.wait_ge(s_pqw, upto(g1, 3 * GROUP, 3 * k + 3))
                    wait(act, pe["qwT"], upto(g1, GROUP, k - 1))
                    if phase == "second" and k == 0:
                        act.wait_ge(s_cleared, 1)
                    for i, blocks in ((0, slice(0, 2)), (1, slice(0, 3, 2))):
                        act.activation(qw_parts[:, k % 2, i, :].rearrange("p (c h) -> p c h", c=3)[:, blocks, 0:H1],
                                       over_heads(pqw[:, k % 2, 1 + i, :], 2), ACT.Copy).then_inc(s_qwhi, 1)
                elif name == "qwTo":
                    act.wait_ge(pe["qwT"], upto(g1, GROUP, k + 1))
                    wait(act, pe["wb"], upto(g1, THIRDS * GROUP, THIRDS * (k - 1)))
                    wait(act, s_rows, upto(g1, GROUP, k - 1))
                    act.activation(qwT[:, k % 2, :, :],
                                   t_bank[t_at("qwT", k, phase)][0:QW_ROWS, 0:2 * P].rearrange("p (i n) -> p i n", i=2),
                                   ACT.Copy).then_inc(s_qwT, 1)
                elif name == "elu":
                    wait(act, s_elu, upto(g1, GROUP, k))
                    act.wait_ge(s_fb, upto(g1, GROUP, k + 1))
                    act.activation(f_neg, f_b[:, k % 2, :], ACT.Relu, scale=-1.0,
                                   bias=minus_one[:]).then_inc(s_fneg, 1)
                    act.wait_ge(s_fneg, upto(g1, GROUP, k + 1))
                    wait(act, s_ex, upto(g1, GROUP, k))
                    act.activation(f_exp, f_neg, ACT.Exp, scale=-1.0).then_inc(s_elu, 1)

            phases(act, step, "ACT")

        @block.vector
        def _(dve):
            dve.memset(h[:, :, :, HD1:HD1 + 1], 1.0)
            dve.memset(eps1[:], LN_EPS / 4)
            dve.memset(minus_one[:], -1.0)
            def prepare_constants():
                dve.wait_ge(s_bias1, 4 * 16)
                dve.tensor_reduce(sd_shift[:, 0, :], w_sd[:, 1, :].rearrange("p (h e) -> p h e", h=H1), AX_X,
                                  ALU.add, apply_absolute_value=True).then_inc(s_shift, 1)
                dve.wait_ge(s_shift, 1)
                dve.tensor_scalar(sd_shift[:, 0, :], sd_shift[:, 0, :], -EXP_ROOM, 0.0, ALU.add,
                                  ALU.max).then_inc(s_shift, 1)
                dve.wait_ge(s_shift, 2)
                dve.tensor_scalar(sd_shift[:, 1, :], sd_shift[:, 0, :], -1.0, None, ALU.mult).then_inc(s_shift, 1)
                dve.wait_ge(s_shift, 3)
                dve.tensor_scalar(bias_1[:], bias_1[:], -1.0, None, ALU.add).then_inc(s_consts, 1)

            def low(dst, src, hi):
                return dve.tensor_tensor(dst, src, hi.bitcast(F32), ALU.subtract)

            sums1 = context1[:, 0:H1 * (HD1 + 1)].rearrange("p (h e) -> p h e", h=H1)

            def step(name, k, g1, phase):
                g0, gx = g1 + 1, g1 + 2
                if name == "wlo":
                    n = WEIGHTS[k]
                    dve.wait_ge(s_whi, k + 1)
                    dve.scalar_tensor_tensor(out=w[n][:, LO], in0=stage_ap[n], scalar=SCALE if n == "q" else 1.0,
                                             in1=w[n][:, HI].bitcast(F32), op0=ALU.mult,
                                             op1=ALU.subtract).then_inc(s_wlo, 1)
                elif name == "glo":
                    dve.wait_ge(s_ghi, k + 1)
                    low(w["g"][:, LO, k, :], context1[:, 0:D], w["g"][:, HI, k, :]).then_inc(s_glo, 1)
                elif name == "outb":
                    dve.wait_ge(s_ob, 1)
                    dve.tensor_tensor(out_bias[:], context1[:, 0:D], bias_f[:], ALU.add).then_inc(s_outb, 1)
                elif name == "consts":
                    prepare_constants()
                elif name == "xlo":
                    dve.wait_ge(s_xhi, upto(gx, GROUP, k + 1))
                    cols = slice(k * P, (k + 1) * P)
                    low(xT[:, LO, :, cols], t_bank[t_at("xT", k, phase)][:, 0:D].rearrange("p (k n) -> p k n", k=KT),
                        xT[:, HI, :, cols]).then_inc(s_xlo, 1)
                elif name == "qklo":
                    dve.wait_ge(s_qkhi, upto(g0, 2 * PAIRS, k + 1))
                    dst = (qT, kT)[k % 2]
                    dve.scalar_tensor_tensor(out=dst[:, LO, k // 2, :], in0=p_bank[p_at("qk", k, phase)][:, :],
                                             scalar=bias_q[:, k % 2, k // 2:k // 2 + 1],
                                             in1=dst[:, HI, k // 2, :].bitcast(F32),
                                             op0=ALU.add, op1=ALU.subtract).then_inc(s_qklo, 1)
                elif name == "mask":
                    dve.wait_ge(pe["s"], upto(g0, GROUP, k + 1))
                    if k == 0:
                        dve.wait_ge(s_neg, upto(g0, 1, 1))
                    wait(dve, s_exp, upto(g0, GROUP, k - 1))
                    dve.tensor_tensor(masked[:, k % 2].rearrange("p (b j) n -> p b j n", b=2),
                                      scores[:, :, 0:PAIRS * P].rearrange("p b (j n) -> p b j n", j=PAIRS),
                                      neg[:, k, :].unsqueeze(1).unsqueeze(1).broadcast_to([P, 2, PAIRS, P]),
                                      ALU.add).then_inc(s_masked, 1)
                elif name == "max":
                    dve.wait_ge(s_masked, upto(g0, GROUP, k + 1))
                    wait(dve, s_exp, upto(g0, GROUP, k))
                    dve.tensor_reduce(neg_max[:], masked[:, k % 2], AX_X, ALU.max, negate=True).then_inc(s_max, 1)
                elif name == "rden0":
                    dve.wait_ge(s_exp, upto(g0, GROUP, k + 1))
                    wait(dve, s_norm, upto(g0, GROUP, k))
                    dve.reciprocal(rden0[:], den0[:, k % 2, :]).then_inc(s_rden0, 1)
                elif name == "clo":
                    dve.wait_ge(s_chi, upto(g0, GROUP, k + 1))
                    low(cT[:, LO], context0[:, 0:D].rearrange("p (k n) -> p k n", k=KT),
                        cT[:, HI]).then_inc(s_clo, 1)
                elif name == "sum0":
                    dve.wait_ge(pe["f"], upto(g0, GROUP, k + 1))
                    dve.wait_ge(s_xb, upto(g0, 1, 1))
                    wait(dve, s_x1, upto(g0, GROUP, k - 1))
                    dve.tensor_tensor(sum0[:, k % 2, :], p_bank[p_at("f", k, phase)][:, 0:D], x_res[:, k, :],
                                      ALU.add).then_inc(s_sum0, 1)
                elif name == "stats0":
                    dve.wait_ge(s_sum0, upto(g0, GROUP, k + 1))
                    dve.bn_stats(stats0[:, k, :], sum0[:, k % 2, :]).then_inc(s_st0, 1)
                elif name == "mv0":
                    dve.wait_ge(s_st0, upto(g0, GROUP, k + 1))
                    dve.sem_inc(s_seen, 1)
                    dve.bn_aggr(mv0[:, k, :], stats0[:, k, :]).then_inc(s_mv0, 1)
                elif name == "x1":
                    dve.wait_ge(s_rstd0, upto(g0, GROUP, k + 1))
                    wait(dve, s_sum1, upto(g1, GROUP, k + 1))
                    if phase == "first" and k == 0:
                        dve.wait_ge(s_wlo, 5)
                    dve.tensor_scalar(x1[:, k, :], sum0[:, k % 2, :], mv0[:, k, 0:1], rstd0[:, k:k + 1],
                                      ALU.subtract, ALU.mult).then_inc(s_x1, 1)
                elif name == "clip":
                    dve.wait_ge(pe["maskT"], upto(g0, 2, k + 1))
                    wait(dve, s_e, upto(g1, THIRDS * GROUP, THIRDS * GROUP))
                    src = t_bank[t_at("maskT", k, phase)][:, 0:P].bitcast(BF16).rearrange("p (i n) -> p i n", i=2)
                    dve.tensor_scalar(clip[:, 2 * k:2 * k + 2, :], src, KEEP, FLOOR, ALU.mult, ALU.add).then_inc(s_mx, 1)
                elif name == "x1lo":
                    dve.wait_ge(s_x1hi, upto(g1, GROUP, k + 1))
                    low(x1T[:, LO], t_bank[t_at("x1T", k, phase)][:, 0:D].rearrange("p (k n) -> p k n", k=KT),
                        x1T[:, HI]).then_inc(s_x1lo, 1)
                elif name == "gsum":
                    dve.wait_ge(pe["gate"], upto(g1, GROUP, k + 1))
                    dve.wait_ge(s_bias1, 4 * 16)
                    wait(dve, s_gate, upto(g1, GROUP, k))
                    dve.tensor_tensor(gate_sum[:], p_bank[p_at("gate", k, phase)][:, 0:D], gate_bias[:],
                                      ALU.add).then_inc(s_gsum, 1)
                elif name == "sd":
                    dve.wait_ge(s_prod, upto(g1, GROUP, k + 1))
                    wait(dve, s_sda, upto(g1, GROUP, k))
                    dve.tensor_reduce(sd[:].rearrange("p a h -> p (a h)"),
                                      prod[:].rearrange("p a (h e) -> p (a h) e", h=H1), AX_X,
                                      ALU.add).then_inc(s_sd, 1)
                elif name == "sda":
                    dve.wait_ge(s_sd, upto(g1, GROUP, k + 1))
                    wait(dve, s_pqw, upto(g1, 3 * GROUP, 3 * k))
                    dve.tensor_tensor(sda[:], sd[:], sd_shift[:], ALU.add).then_inc(s_sda, 1)
                elif name == "wlog":
                    dve.wait_ge(s_sda, upto(g1, GROUP, k + 1))
                    dve.tensor_scalar(wlog[:], sda[:, 0, :], -EXP_ROOM, None, ALU.max).then_inc(s_wlog, 1)
                elif name == "qwlo":
                    dve.wait_ge(s_qwhi, upto(g1, 2 * GROUP, 2 * k + 2))
                    parts = qw_parts[:, k % 2, :, :].rearrange("p i c -> p (i c)")
                    lo = parts[:, 2 * BLOCK:6 * BLOCK].rearrange("p (i c) -> p i c", i=2)[:, :, 0:H1]
                    low(lo, pqw[:, k % 2, 1:3, :], qw_parts[:, k % 2, :, 0:H1]).then_inc(s_qwlo, 1)
                elif name == "e":
                    g, r = divmod(k, THIRDS)
                    dve.wait_ge(pe["wb"], upto(g1, THIRDS * GROUP, k + 1))
                    if phase == "second" and k == 0:
                        dve.wait_ge(s_wlo, 5)
                    wait(dve, pe["pv1"], upto(g1, THIRDS * GROUP, k + 1 - THIRDS))
                    src = t_bank[t_at("wb", k, phase)]
                    for i in range(H1 // THIRDS):
                        n = H1 // THIRDS * r + i
                        last = dve.scalar_tensor_tensor(out=weights[:, n, :], in0=src[:, i * P:(i + 1) * P],
                                                        scalar=pqw[:, g % 2, 0, n:n + 1], in1=clip[:, g, :],
                                                        op0=ALU.max, op1=ALU.min)
                    last.then_inc(s_e, 1)
                elif name == "rden1":
                    dve.wait_ge(pe["pv1"], upto(g1, THIRDS * GROUP, THIRDS * (k + 1)))
                    dve.reciprocal(rden1[:], sums1[:, :, HD1:HD1 + 1].rearrange("p h o -> p (h o)")).then_inc(s_rden1, 1)
                elif name == "f_raw":
                    dve.wait_ge(s_rden1, upto(g1, GROUP, k + 1))
                    wait(dve, s_fb, upto(g1, GROUP, k))
                    dve.tensor_tensor(f_raw[:].rearrange("p (h e) -> p h e", h=H1), sums1[:, :, 0:HD1],
                                      per_head(rden1[:], HD1), ALU.mult).then_inc(s_fraw, 1)
                elif name == "mixa":
                    dve.wait_ge(s_ex, upto(g1, GROUP, k + 1))
                    wait(dve, s_sum1, upto(g1, GROUP, k))
                    dve.scalar_tensor_tensor(out=mix[:], in0=f_b[:, k % 2, :], scalar=-1.0, in1=exp_less_x,
                                             op0=ALU.max, op1=ALU.add).then_inc(s_mixa, 1)
                elif name == "mixb":
                    dve.wait_ge(s_mixa, upto(g1, GROUP, k + 1))
                    dve.wait_ge(s_gate, upto(g1, GROUP, k + 1))
                    dve.scalar_tensor_tensor(out=mix[:], in0=gate_t[:, k % 2, :], scalar=1.0, in1=mix[:],
                                             op0=ALU.add, op1=ALU.mult).then_inc(s_mixb, 1)
                elif name == "sum1":
                    dve.wait_ge(s_mixb, upto(g1, GROUP, k + 1))
                    wait(dve, s_y, upto(g1, GROUP, k - 1))
                    dve.scalar_tensor_tensor(out=sum1[:, k % 2, :], in0=mix[:], scalar=0.25, in1=x1[:, k, :],
                                             op0=ALU.mult, op1=ALU.add).then_inc(s_sum1, 1)
                elif name == "stats1":
                    dve.wait_ge(s_sum1, upto(g1, GROUP, k + 1))
                    dve.bn_stats(stats1[:, k, :], sum1[:, k % 2, :]).then_inc(s_st1, 1)
                elif name == "mv1":
                    dve.wait_ge(s_st1, upto(g1, GROUP, k + 1))
                    dve.sem_inc(s_seen, 1)
                    dve.bn_aggr(mv1[:, k, :], stats1[:, k, :]).then_inc(s_mv1, 1)
                elif name == "out":
                    dve.wait_ge(s_rstd1, upto(g1, GROUP, k + 1))
                    wait(dve, s_store[k % 2], upto(g1, GROUP // 2 * 16, k // 2 * 16))
                    dve.tensor_scalar(y_out[:, k % 2, :], sum1[:, k % 2, :], mv1[:, k, 0:1], rstd1[:, k:k + 1],
                                      ALU.subtract, ALU.mult).then_inc(s_y, 1)

            phases(dve, step, "DVE")

        @block.gpsimd
        def _(pool):
            pool.memset(ident[:], 0.0).then_inc(s_const, 1)
            pool.memset(eps0[:], LN_EPS).then_inc(s_const, 1)
            pool.memset(minus_half[:], -0.5).then_inc(s_const, 1)
            pool.wait_ge(s_const, 3)
            pool.affine_select(out=ident[:], in_=ident[:], compare_op=ALU.not_equal, fill=1.0, base=0,
                               pattern=[[-1, P]], channel_multiplier=1).then_inc(s_const, 1)
            pool.memset(qw_parts[:].bitcast(F32), 0.0).then_inc(s_cleared, 1)
            pool.memset(own_head[:], 0.0).then_inc(s_head, 1)
            for c in range(3):
                pool.wait_ge(s_head, c + 1)
                pool.affine_select(out=own_head[:], in_=own_head[:], compare_op=ALU.not_equal, fill=1.0,
                                   base=-BLOCK * c, pattern=[[-1, H1]], channel_multiplier=1).then_inc(s_head, 1)

            def rsqrt(mv, ve, rstd, eps, made_mv, made_ve, made_rstd, n):
                pool.wait_ge(made_mv, n)
                pool.tensor_tensor(ve, mv, eps[:], ALU.add).then_inc(made_ve, 1)
                pool.wait_ge(made_ve, n)
                pool.tensor_tensor(rstd, ve, minus_half[:], ALU.pow).then_inc(made_rstd, 1)

            def step(name, k, g1, phase):
                g0, gx = g1 + 1, g1 + 2
                if name == "x_res":
                    pool.wait_ge(s_x, upto(g0, 16, 16))
                    if phase == "first":
                        pool.wait_ge(s_outb, 1)
                        pool.wait_ge(s_wlo, 3)
                    wait(pool, s_sum0, upto(g0, GROUP, 0))
                    pool.tensor_tensor(x_res[:], x_in[:], over_heads(out_bias[:], GROUP), ALU.add).then_inc(s_xb, 1)
                elif name == "norm":
                    pool.wait_ge(s_rden0, upto(g0, GROUP, k + 1))
                    probs = probs0[:, k % 2].rearrange("p b (j n) -> p (b j) n", j=PAIRS)
                    pool.tensor_tensor(probs, probs, per_head(rden0[:], P), ALU.mult).then_inc(s_norm, 1)
                elif name == "rstd0":
                    if phase == "first" and k == 0:
                        pool.wait_ge(s_table, 1)
                    rsqrt(mv0[:, k, 1:2], ve0[:, k:k + 1], rstd0[:, k:k + 1], eps0, s_mv0, s_ve0, s_rstd0,
                          upto(g0, GROUP, k + 1))
                elif name == "prod":
                    pool.wait_ge(s_th, upto(g1, GROUP, k + 1))
                    wait(pool, s_sd, upto(g1, GROUP, k))
                    if phase == "second" and k == 0:
                        pool.wait_ge(s_consts, 1)
                    pool.tensor_tensor(prod[:], over_heads(th[:], 2), w_sd[:], ALU.mult).then_inc(s_prod, 1)
                elif name == "rows":
                    pool.wait_ge(s_qwT, upto(g1, GROUP, k + 1))
                    wait(pool, pe["wb"], upto(g1, THIRDS * GROUP, THIRDS * (k - 1)))
                    if phase == "second" and k == 0:
                        pool.wait_ge(s_head, 4)
                    pool.tensor_tensor(w_rows[0:QW_ROWS, k % 2], over_heads(qwT[:, k % 2, 1, :].bitcast(F32), H1),
                                       per_head(own_head[:], P), ALU.mult).then_inc(s_rows, 1)
                elif name == "fb":
                    pool.wait_ge(s_fraw, upto(g1, GROUP, k + 1))
                    wait(pool, s_mixb, upto(g1, GROUP, k - 1))
                    pool.tensor_tensor(f_b[:, k % 2, :].rearrange("p (h e) -> p h e", h=H1),
                                       f_raw[:].rearrange("p (h e) -> p h e", h=H1),
                                       over_heads(bias_1[:], H1), ALU.add).then_inc(s_fb, 1)
                elif name == "ex":
                    pool.wait_ge(s_elu, upto(g1, GROUP, k + 1))
                    wait(pool, s_mixb, upto(g1, GROUP, k))
                    pool.tensor_tensor(exp_less_x, f_exp, x1[:, k, :], ALU.subtract).then_inc(s_ex, 1)
                elif name == "rstd1":
                    rsqrt(mv1[:, k, 1:2], ve1[:, k:k + 1], rstd1[:, k:k + 1], eps1, s_mv1, s_ve1, s_rstd1,
                          upto(g1, GROUP, k + 1))

            phases(pool, step, "POOL")


T_STAGES = {"pT", "qwT", "xT", "x1T", "wb", "maskT"}
P_STAGES = {"qk", "v", "f", "h", "gate"}


def bank_uses(stages, phase):
    return [(n, k) for n, k in ORDERS[phase]["PE"] if n in stages]


def t_at(name, k, phase):
    return bank_uses(T_STAGES, phase).index((name, k)) % 2


def p_at(name, k, phase):
    return bank_uses(P_STAGES, phase).index((name, k)) % 2


_INS = ['x', 'adj', 'L0_gnn_Wq', 'L0_gnn_bq', 'L0_gnn_Wk', 'L0_gnn_bk', 'L0_gnn_Wv', 'L0_gnn_bv', 'L0_gnn_Wf',
        'L0_gnn_bf', 'L1_gnn_W', 'L1_gnn_b', 'L1_gnn_w_src', 'L1_gnn_w_dst', 'L1_gnn_H_w', 'L1_gnn_H_b']
_OUTS = [((64, 128, 384), 'float32')]


def kernel(**inputs):
    import numpy as _np
    import concourse.bacc as _bacc
    from concourse import mybir as _mybir
    from concourse.bass_utils import run_bass_kernel_spmd as _run

    nc = _bacc.Bacc("TRN2", target_bir_lowering=False, num_devices=1)
    arrays, args = {}, []
    for name in _INS:
        a = _np.ascontiguousarray(inputs[name])
        arrays[f"in_{name}_dram"] = a
        args.append(nc.dram_tensor(f"in_{name}_dram", a.shape, _mybir.dt.from_np(a.dtype), kind="ExternalInput").ap())
    for i, (shape, dtype) in enumerate(_OUTS):
        dt = _mybir.dt.from_np(_np.dtype(dtype))
        args.append(nc.dram_tensor(f"out_{i}_dram", shape, dt, kind="ExternalOutput").ap())
    bass_graph_transformer_gat(nc, *args)
    r = _run(nc, [arrays], core_ids=[0])
    got = tuple(r.results[0][f"out_{i}_dram"] for i in range(len(_OUTS)))
    return got[0]
```
